# Optimizing a Trainium2 kernel written in Bass

```python
import numpy as np
import jax
import jax.numpy as jnp

def _softmax(x, axis=-1):
    return jax.nn.softmax(x, axis=axis)

def _gelu(x):
    return jax.nn.gelu(x, approximate=True)

def _silu(x):
    return jax.nn.silu(x)

def _sigmoid(x):
    return jax.nn.sigmoid(x)

def _layernorm(x, axis=-1, eps=1e-05):
    m = jnp.mean(x, axis=axis, keepdims=True)
    v = jnp.var(x, axis=axis, keepdims=True)
    return (x - m) / jnp.sqrt(v + eps)

def _scatter_add(tgt, idx, src, axis=0):
    return tgt.at[idx].add(src)

def _segment_sum(src, seg, n):
    return jax.ops.segment_sum(src, seg, n)
kernel_name = 'mk_gnn_ffn_d1_gnn_r8_54cc2d'

def setup_inputs(seed: int=0):
    np.random.seed(seed)
    _w = jnp.asarray

    def _rec_inputs():
        import jax
        import jax.numpy as jnp
        _gk = jax.random.key(seed)
        x = -0.0002117 + 1 * jax.random.normal(jax.random.fold_in(_gk, 1), (12500, 256), jnp.float32)
        _s = jax.random.randint(jax.random.fold_in(_gk, 2), (100000,), 0, 12500, jnp.int32)
        _d = jax.random.randint(jax.random.fold_in(_gk, 3), (100000,), 0, 12500, jnp.int32)
        _loop = jnp.arange(12500, dtype=jnp.int32)
        src = jnp.concatenate([_s, _d, _loop])
        dst = jnp.concatenate([_d, _s, _loop])
        _o = jnp.argsort(dst, stable=True)
        src = src[_o]
        dst = dst[_o]
        edge_weight = jax.random.uniform(jax.random.fold_in(_gk, 12), (212500,), jnp.float32, 0.0, 1)
        return (x, src, dst, edge_weight)
    x, src, dst, edge_weight = _rec_inputs()

    def _L0_gnn_setup():
        import jax, jax.numpy as jnp
        import numpy as np
        N_NODES = 12500
        N_EDGES = 400000
        IN_FEATS = 256
        OUT_FEATS = 256
        key = jax.random.key(seed)
        k1, k2, k3, k4, k5, k6 = jax.random.split(key, 6)
        features = jax.random.normal(k1, (N_NODES, IN_FEATS), dtype=jnp.float32)
        edge_src = jax.random.randint(k2, (N_EDGES,), 0, N_NODES, dtype=jnp.int64)
        edge_dst = jnp.sort(jax.random.randint(k3, (N_EDGES,), 0, N_NODES, dtype=jnp.int64))
        edge_weight = jax.random.uniform(k4, (N_EDGES,), dtype=jnp.float32)
        bound = 1.0 / np.sqrt(IN_FEATS)
        W = jax.random.uniform(k5, (OUT_FEATS, IN_FEATS), dtype=jnp.float32, minval=-bound, maxval=bound)
        b = jax.random.uniform(k6, (OUT_FEATS,), dtype=jnp.float32, minval=-bound, maxval=bound)
        return {'features': features, 'edge_src': edge_src, 'edge_dst': edge_dst, 'edge_weight': edge_weight, 'W': W, 'b': b}
    _L0_gnn_all = _L0_gnn_setup()
    _L0_gnn_in = {k: v for k, v in _L0_gnn_all.items() if k in ('W', 'b')}
    del _L0_gnn_all

    def _L0_ffn_setup():
        import jax, jax.numpy as jnp
        import numpy as np
        B, T, D, H, E = (16, 512, 256, 512, 8)
        key = jax.random.key(seed)
        ks = jax.random.split(key, 5)
        x = jax.random.normal(ks[0], (B, T, D), dtype=jnp.float32)
        gate_w = jax.random.normal(ks[1], (D, E), dtype=jnp.float32) * 0.02
        gate_b = jnp.zeros((E,), dtype=jnp.float32)
        W1 = jax.random.normal(ks[2], (E, D, H), dtype=jnp.float32) * 0.02
        b1 = jnp.zeros((E, H), dtype=jnp.float32)
        W2 = jax.random.normal(ks[3], (E, H, D), dtype=jnp.float32) * 0.02
        b2 = jnp.zeros((E, D), dtype=jnp.float32)
        return {'x': x, 'gate_w': gate_w, 'gate_b': gate_b, 'W1': W1, 'b1': b1, 'W2': W2, 'b2': b2}
    _L0_ffn_all = _L0_ffn_setup()
    _L0_ffn_in = {k: v for k, v in _L0_ffn_all.items() if k in ('gate_w', 'gate_b', 'W1', 'b1', 'W2', 'b2')}
    del _L0_ffn_all
    return {'x': x, 'src': src, 'dst': dst, 'edge_weight': edge_weight, 'L0_gnn_W': _L0_gnn_in['W'], 'L0_gnn_b': _L0_gnn_in['b'], 'L0_ffn_gate_w': _L0_ffn_in['gate_w'], 'L0_ffn_gate_b': _L0_ffn_in['gate_b'], 'L0_ffn_W1': _L0_ffn_in['W1'], 'L0_ffn_b1': _L0_ffn_in['b1'], 'L0_ffn_W2': _L0_ffn_in['W2'], 'L0_ffn_b2': _L0_ffn_in['b2']}

def reference(x, src, dst, edge_weight, L0_gnn_W, L0_gnn_b, L0_ffn_gate_w, L0_ffn_gate_b, L0_ffn_W1, L0_ffn_b1, L0_ffn_W2, L0_ffn_b2):
    import jax
    import jax.numpy as jnp

    def _L0_gnn_ref(features, edge_src, edge_dst, edge_weight, W, b):
        import jax, jax.numpy as jnp
        import numpy as np
        N_NODES = 12500
        N_EDGES = 400000
        IN_FEATS = 256
        OUT_FEATS = 256
        msgs = features[edge_src] * edge_weight[:, None]
        agg = jax.ops.segment_sum(msgs, edge_dst, num_segments=N_NODES, indices_are_sorted=True)
        return jnp.einsum('ni,oi->no', agg, W) + b

    def _L0_ffn_ref(x, gate_w, gate_b, W1, b1, W2, b2):
        import jax, jax.numpy as jnp
        import numpy as np
        B, T, D, H, E = (16, 512, 256, 512, 8)
        Bb, Tt, Dd = x.shape
        Ee = gate_w.shape[1]
        xf = x.reshape(-1, Dd)
        N = xf.shape[0]
        logits = xf @ gate_w + gate_b
        probs = jax.nn.softmax(logits, axis=-1)
        top2_vals, top2_idx = jax.lax.top_k(probs, 2)
        cw = jnp.zeros((N, Ee), dtype=xf.dtype).at[jnp.arange(N)[:, None], top2_idx].add(top2_vals)

        def step(acc, params):
            w1, bb1, w2, bb2, we = params
            h = jax.nn.gelu(xf @ w1 + bb1, approximate=False)
            y = h @ w2 + bb2
            return (acc + we[:, None] * y, None)
        out, _ = jax.lax.scan(step, jnp.zeros_like(xf), (W1, b1, W2, b2, cw.T))
        return out.reshape(Bb, Tt, Dd)
    x = x + _L0_gnn_ref(_layernorm(x, axis=-1), src, dst, edge_weight, L0_gnn_W, L0_gnn_b)
    x = x + _L0_ffn_ref(_layernorm(x, axis=-1)[None], L0_ffn_gate_w, L0_ffn_gate_b, L0_ffn_W1, L0_ffn_b1, L0_ffn_W2, L0_ffn_b2)[0]
    return x

_drawn_inputs = setup_inputs


def setup_inputs(seed=0):
    import zlib

    import numpy as np

    out = dict(_drawn_inputs(seed))
    spreads = {'L0_ffn_gate_b': (0.0, 0.717), 'L0_ffn_b1': (0.0, 0.8), 'L0_ffn_b2': (0.0, 0.53)}
    factors = {'L0_ffn_gate_w': 3.351, 'L0_ffn_W1': 4.832, 'L0_ffn_W2': 4.543}
    for name, (base, spread) in spreads.items():
        noise = np.random.default_rng([zlib.crc32(name.encode()), seed]).standard_normal(out[name].shape)
        drawn = base * np.exp(spread * noise) if base else spread * noise
        out[name] = jnp.asarray(drawn.astype(out[name].dtype))
    for name, factor in factors.items():
        out[name] = (out[name] * factor).astype(out[name].dtype)
    return out
```

```python
from contextlib import ExitStack

import concourse.bass as bass
from concourse import mybir

F32 = mybir.dt.float32
I32 = mybir.dt.int32
U16 = mybir.dt.uint16
ALU = mybir.AluOpType
ACT = mybir.ActivationFunctionType
AX = mybir.AxisListType

P = 128
N, D = 12500, 256
E_EDGES = 212500
NX, H = 8, 512
KD = D // P
KH = H // P
EPS = 1e-5

CG = 8
GROUP = CG * P
NG = -(-E_EDGES // GROUP)
NG += NG % 2
NCH = NG * CG
FULL_CHUNKS = E_EDGES // P
REST_EDGES = E_EDGES - FULL_CHUNKS * P
CB = NCH // P
CB_FULL = FULL_CHUNKS // P
assert CB * P == NCH and CB_FULL == CB - 1
LAST_ROWS = FULL_CHUNKS - CB_FULL * P
W = 80
WG = 64
MAX_WINDOWS = NG + N // WG + 1

NT = -(-N // P)
LAST = N - (NT - 1) * P
NPAD = NT * P

LB = 8
LJ = N // P
NLB = LJ // LB
LREST = N - LJ * P
LBUF = 4
assert LJ == NLB * LB + 1 and NLB % LBUF == 0

IT = 256
TB = IT // P
PARTS = ((0, 28), (28, 56), (56, 78), (78, NT))
NTM = max(t1 - t0 for t0, t1 in PARTS)


def n_items(t0, t1):
    pairs = 2 * (min(t1 * P, N) - t0 * P)
    n = (pairs + NX * (IT - 1)) // IT
    return n + n % 2


ITEMS = [n_items(*p) for p in PARTS]
FIRST = [sum(ITEMS[:k]) for k in range(len(PARTS) + 1)]
NI = FIRST[-1]


def build(nc, x, src, dst, edge_weight, gnn_w, gnn_b, gate_w, gate_b, w1, b1, w2, b2, out):
    xhat = nc.dram_tensor("xhat", (N, D), F32, kind="Internal").ap()
    slots_x = [nc.dram_tensor(f"slots_x{k}", (n * IT, D), F32, kind="Internal").ap() for k, n in enumerate(ITEMS)]
    slots_y = [nc.dram_tensor(f"slots_y{k}", (n * IT, D), F32, kind="Internal").ap() for k, n in enumerate(ITEMS)]
    b1_cols = nc.dram_tensor("b1_cols", (NX, P, KH), F32, kind="Internal").ap()
    with ExitStack() as mem:
        sb = lambda name, shape, dt=F32: mem.enter_context(nc.sbuf_tensor(name, shape, dt))
        m = {
            "acc": sb("acc", [P, KD, NPAD + W]),
            "ident": sb("ident", [P, P]),
            "gnn_wT": sb("gnn_wT", [P, KD, D]),
            "gate_wS": sb("gate_wS", [P, KD, NX]),
            "gate_bB": sb("gate_bB", [P, NX]),
            "gnn_bB": sb("gnn_bB", [P, D]),
            "eps": sb("eps", [P, 1]),
            "dst_rel": sb("dst_rel", [P, NCH + 2 * CG], U16),
            "src_t": sb("src_t", [P, NCH + 2 * CG], U16),
            "wgt": sb("wgt", [P, NCH + 2 * CG]),
            "last_rel": sb("last_rel", [1, NG], I32),
            "base_i": sb("base_i", [1, NG], I32),
            "wide": sb("wide", [1, 1], I32),
            "iota_w": sb("iota_w", [P, W]),
            "bank": [mem.enter_context(nc.psum_tensor(f"bank{i}", [P, 512], F32)) for i in range(8)],
        }
        prepare(nc, m, x, src, dst, edge_weight, gnn_w, gnn_b, gate_w, gate_b, b1, b1_cols, xhat)
        layers(nc, m, x, xhat, w1, b1_cols, w2, b2, slots_x, slots_y, out)


def prepare(nc, m, x, src, dst, edge_weight, gnn_w, gnn_b, gate_w, gate_b, b1, b1_cols, xhat):
    ident, bank = m["ident"], m["bank"]
    with ExitStack() as s:
        sb = lambda name, shape, dt=F32: s.enter_context(nc.sbuf_tensor("pre_" + name, shape, dt))
        sem = lambda name: s.enter_context(nc.semaphore("pre_" + name))
        dst_raw = sb("dst_raw", [P, CB, P], I32)
        src_raw = sb("src_raw", [P, CB, P], I32)
        wgt_raw = sb("wgt_raw", [P, CB, P])
        dst_f, src_f = sb("dst_f", [P, CB, P]), sb("src_f", [P, CB, P])
        base_b = sb("base_b", [P, NG])
        last_i = sb("last_i", [1, NG], I32)
        base_f, span_f, span_max, wide_f = sb("base_f", [1, NG]), sb("span_f", [1, NG]), sb("span_max", [1, 1]), sb("wide_f", [1, 1])
        ones_row = sb("ones_row", [1, P])
        gnn_raw = sb("gnn_raw", [P, KD, D])
        b1_raw = sb("b1_raw", [NX, H])
        b1_t = sb("b1_t", [P, NX, KH])
        rows = [sb(f"rows{i}", [P, LB, D]) for i in range(LBUF)]
        stats = [sb(f"stats{i}", [P, LB, 6]) for i in range(2)]
        mv = [sb(f"mv{i}", [P, LB, 2]) for i in range(LBUF)]
        var_eps, rstd = ([sb(f"{n}{i}", [P, LB]) for i in range(LBUF)] for n in ("var_eps", "rstd"))
        mean_rstd, shift = ([sb(f"{n}{i}", [P, LB]) for i in range(LBUF)] for n in ("mean_rstd", "shift"))
        eps8, half8, minus8 = sb("eps8", [P, LB]), sb("half8", [P, LB]), sb("minus8", [P, LB])
        pad_set, zero_set, ident_set, consts = sem("pad_set"), sem("zero_set"), sem("ident_set"), sem("consts")
        edges_in, base_in, params_in = sem("edges_in"), sem("base_in"), sem("params_in")
        as_float, turned, turned_out, params_turned = sem("as_float"), sem("turned"), sem("turned_out"), sem("params_turned")
        dve_step, b1_ready, b1_stored = sem("dve_step"), sem("b1_ready"), sem("b1_stored")
        loaded = [sem(f"loaded{i}") for i in range(LBUF)]
        stored = [sem(f"stored{i}") for i in range(LBUF)]
        stats_done, stats_seen, mv_ready = sem("stats_done"), sem("stats_seen"), sem("mv_ready")
        base_spread, base_b_set = sem("base_spread"), sem("base_b_set")
        pow_step, coef_ready, norm_done = sem("pow_step"), sem("coef_ready"), sem("norm_done")

        x_main = x[0:P * LJ].rearrange("(p j) f -> p j f", p=P)
        h_main = xhat[0:P * LJ].rearrange("(p j) f -> p j f", p=P)
        turns = [(k, b, min(4, CB - b)) for k in range(3) for b in range(0, CB, 4)]
        tail_rows = (P, LREST)
        block = s.enter_context(nc.Block())

        @block.gpsimd
        def _(pool):
            nc.gpsimd.memset(dst_raw[:, CB - 1, :], 40000)
            nc.gpsimd.memset(src_raw[:, CB - 1, :], 0)
            nc.gpsimd.memset(wgt_raw[:, CB - 1, :], 0.0).then_inc(pad_set, 1)
            nc.gpsimd.memset(ident[:], 0.0).then_inc(zero_set, 1)
            nc.gpsimd.memset(eps8[:], EPS)
            nc.gpsimd.memset(half8[:], -0.5)
            nc.gpsimd.memset(minus8[:], -1.0)
            nc.gpsimd.memset(ones_row[:], 1.0)
            pool.wait_ge(zero_set, 1)
            pool.affine_select(out=ident[:], in_=ident[:], compare_op=ALU.not_equal, fill=1.0, base=0,
                               pattern=[[-1, P]], channel_multiplier=1).then_inc(ident_set, 1)
            nc.gpsimd.iota(m["iota_w"][:], pattern=[[1, W]], base=0, channel_multiplier=0,
                           allow_small_or_imprecise_dtypes=True)
            nc.gpsimd.memset(m["src_t"][:, NCH:], 0)
            nc.gpsimd.memset(m["dst_rel"][:, NCH:], 0)
            nc.gpsimd.memset(m["wgt"][:, NCH:], 0.0)
            nc.gpsimd.memset(m["eps"][:], EPS).then_inc(consts, 1)
            pool.wait_ge(consts, 1)

            def coefficients(b, q):
                pool.wait_ge(mv_ready, b + 3)
                nc.gpsimd.tensor_tensor(var_eps[q][:], mv[q][:, :, 1], eps8[:], op=ALU.add).then_inc(pow_step, 1)
                pool.wait_ge(pow_step, b * 3 + 1)
                nc.gpsimd.tensor_tensor(rstd[q][:], var_eps[q][:], half8[:], op=ALU.pow).then_inc(pow_step, 1)
                pool.wait_ge(pow_step, b * 3 + 2)
                nc.gpsimd.tensor_tensor(mean_rstd[q][:], mv[q][:, :, 0], rstd[q][:], op=ALU.mult).then_inc(pow_step, 1)
                pool.wait_ge(pow_step, b * 3 + 3)
                nc.gpsimd.tensor_tensor(shift[q][:], mean_rstd[q][:], minus8[:], op=ALU.mult).then_inc(coef_ready, 1)

            with pool.Fori(0, NLB // LBUF) as i:
                for q in range(LBUF):
                    coefficients(i * LBUF + q, q)
            coefficients(NLB, 0)
            nc.gpsimd.memset(m["acc"][:], 0.0).then_inc(consts, 1)

        @block.sync
        def _(sp):
            full = CB_FULL * P * P
            arrays = ((dst_raw, dst), (src_raw, src), (wgt_raw, edge_weight))
            dst_row = dst.rearrange("(o n) -> o n", o=1)

            def load(b):
                sp.dma_start(rows[b % LBUF][:], x_main[:, b * LB:(b + 1) * LB, :]).then_inc(loaded[b % LBUF], 16)

            load(0)
            load(1)
            for raw, e in arrays:
                sp.dma_start(raw[:, 0:CB_FULL, :],
                             e[0:full].rearrange("(b p e) -> p b e", p=P, e=P)).then_inc(edges_in, 16)
            sp.wait_ge(pad_set, 1)
            for raw, e in arrays:
                body = e[full:FULL_CHUNKS * P].rearrange("(p e) -> p e", e=P)
                sp.dma_start(raw[0:LAST_ROWS, CB - 1, :], body).then_inc(edges_in, 16)
                rest = e[FULL_CHUNKS * P:E_EDGES].rearrange("(p e) -> p e", p=1)
                sp.dma_start(raw[LAST_ROWS:LAST_ROWS + 1, CB - 1, 0:REST_EDGES], rest).then_inc(edges_in, 16)
            sp.dma_start(m["base_i"][:], dst_row[:, 0:E_EDGES:GROUP], allow_slow_non_contiguous=True).then_inc(base_in, 16)
            sp.dma_start(last_i[:, 0:NG - 1], dst_row[:, GROUP - 1:E_EDGES:GROUP],
                         allow_slow_non_contiguous=True).then_inc(base_in, 16)
            sp.dma_start(last_i[:, NG - 1:NG], dst_row[:, E_EDGES - 1:E_EDGES]).then_inc(base_in, 16)
            load(2)
            for to, a in ((gnn_raw[:], gnn_w.rearrange("(b p) i -> p b i", p=P)), (b1_raw[:], b1),
                          (m["gate_wS"][:], gate_w.rearrange("(b p) e -> p b e", p=P)),
                          (m["gate_bB"][:], gate_b.partition_broadcast(P)),
                          (m["gnn_bB"][:], gnn_b.partition_broadcast(P))):
                sp.dma_start(to, a).then_inc(params_in, 16)
            for b in range(NLB):
                q = b % LBUF
                sp.wait_ge(norm_done, b + 1)
                sp.dma_start(h_main[:, b * LB:(b + 1) * LB, :], rows[q][:]).then_inc(stored[q], 16)
                nxt = b + LBUF - 1
                if nxt >= LBUF and nxt <= NLB:
                    sp.wait_ge(stored[nxt % LBUF], nxt // LBUF * 16)
                if nxt < NLB:
                    load(nxt)
                elif nxt == NLB:
                    sp.dma_start(rows[0][:, 0, :], x_main[:, LJ - 1, :]).then_inc(loaded[0], 16)
                    sp.dma_start(rows[0][0:LREST, 1, :], x[P * LJ:N]).then_inc(loaded[0], 16)
            sp.wait_ge(norm_done, NLB + 1)
            sp.dma_start(h_main[:, LJ - 1, :], rows[0][:, 0, :]).then_inc(stored[0], 16)
            sp.dma_start(xhat[P * LJ:N], rows[0][0:LREST, 1, :]).then_inc(stored[0], 16)
            sp.wait_ge(b1_ready, 1)
            sp.dma_start(b1_cols.rearrange("e p k -> p e k"), b1_t[:]).then_inc(b1_stored, 16)
            for q in range(LBUF):
                sp.wait_ge(stored[q], (NLB // LBUF + 2 * (q == 0)) * 16)
            sp.wait_ge(params_in, 5 * 16)
            sp.wait_ge(b1_stored, 16)

        @block.tensor
        def _(pe):
            pe.wait_ge(ident_set, 1)
            pe.wait_ge(as_float, 3)
            pe.wait_ge(consts, 1)
            nc.tensor.matmul(bank[2][:, 0:NG], ones_row[:], base_f[:], start=True, stop=True).then_inc(base_spread, 1)
            for t, (k, b0, nb) in enumerate(turns):
                raw = (dst_f, src_f, wgt_raw)[k]
                if t >= 2:
                    pe.wait_ge(turned_out, t - 1)
                for j in range(nb):
                    last = nc.tensor.transpose(bank[t % 2][:, j * P:(j + 1) * P], raw[:, b0 + j, :], ident[:])
                last.then_inc(turned, 1)
            pe.wait_ge(params_in, 5 * 16)
            for ib in range(KD):
                for ob in range(KD):
                    last = nc.tensor.transpose(bank[3][:, (ib * KD + ob) * P:(ib * KD + ob + 1) * P],
                                               gnn_raw[:, ob, ib * P:(ib + 1) * P], ident[:])
            for hb in range(KH):
                last = nc.tensor.transpose(bank[4][:, hb * NX:(hb + 1) * NX],
                                           b1_raw[:, hb * P:(hb + 1) * P], ident[0:NX, 0:NX])
            last.then_inc(params_turned, 1)

        @block.vector
        def _(dve):
            dve.sem_inc(mv_ready, 2)
            dve.wait_ge(edges_in, 9 * 16)
            nc.vector.tensor_copy(dst_f[:], dst_raw[:]).then_inc(as_float, 1)
            nc.vector.tensor_copy(src_f[:], src_raw[:]).then_inc(as_float, 1)
            dve.wait_ge(base_in, 3 * 16)
            nc.vector.tensor_copy(base_f[:], m["base_i"][:]).then_inc(as_float, 1)
            nc.vector.tensor_tensor(m["last_rel"][:], last_i[:], m["base_i"][:], op=ALU.subtract).then_inc(dve_step, 1)
            nc.vector.tensor_tensor(span_f[:], last_i[:], m["base_i"][:], op=ALU.subtract).then_inc(dve_step, 1)
            dve.wait_ge(dve_step, 2)
            nc.vector.tensor_reduce(span_max[:], span_f[:], axis=AX.X, op=ALU.max).then_inc(dve_step, 1)
            dve.wait_ge(dve_step, 3)
            nc.vector.tensor_scalar(wide_f[:], span_max[:], float(W), None, op0=ALU.is_ge).then_inc(dve_step, 1)
            dve.wait_ge(dve_step, 4)
            nc.vector.tensor_copy(m["wide"][:], wide_f[:])
            dve.wait_ge(base_spread, 1)
            nc.vector.tensor_copy(base_b[:], bank[2][:, 0:NG]).then_inc(base_b_set, 1)
            dve.wait_ge(base_b_set, 1)
            for t, (k, b0, nb) in enumerate(turns):
                dve.wait_ge(turned, t + 1)
                cols = slice(b0 * P, (b0 + nb) * P)
                if k == 0:
                    g0 = b0 * P // CG
                    ng = nb * P // CG
                    nc.vector.tensor_tensor(m["dst_rel"][:, cols].rearrange("p (g c) -> p g c", c=CG),
                                            bank[t % 2][:, 0:nb * P].rearrange("p (g c) -> p g c", c=CG),
                                            base_b[:, g0:g0 + ng].unsqueeze(2).to_broadcast([P, ng, CG]),
                                            op=ALU.subtract).then_inc(turned_out, 1)
                elif k == 1:
                    nc.vector.tensor_copy(m["src_t"][:, cols], bank[t % 2][:, 0:nb * P]).then_inc(turned_out, 1)
                else:
                    nc.vector.tensor_copy(m["wgt"][:, cols], bank[t % 2][:, 0:nb * P]).then_inc(turned_out, 1)

            def moments(b, q, n_rows):
                dve.wait_ge(mv_ready, b + 1)
                for j, n in enumerate(n_rows):
                    last = nc.vector.bn_stats(stats[q % 2][0:n, j, :], rows[q][0:n, j, :])
                last.then_inc(stats_done, 1)
                dve.wait_ge(stats_done, b + 1)
                dve.sem_inc(stats_seen, 1)
                for j, n in enumerate(n_rows):
                    last = nc.vector.bn_aggr(mv[q][0:n, j, :], stats[q % 2][0:n, j, :])
                last.then_inc(mv_ready, 1)

            with dve.Fori(0, NLB // LBUF) as i:
                for q in range(LBUF):
                    dve.wait_ge(loaded[q], i * 16 + 16)
                    moments(i * LBUF + q, q, [P] * LB)
            nc.vector.memset(mv[0][:], 1.0).then_inc(dve_step, 1)
            dve.wait_ge(dve_step, 5)
            dve.wait_ge(loaded[0], (NLB // LBUF + 2) * 16)
            moments(NLB, 0, tail_rows)
            dve.wait_ge(params_turned, 1)
            nc.vector.tensor_copy(m["gnn_wT"][:].rearrange("p b o -> p (b o)"), bank[3][:])
            nc.vector.tensor_copy(b1_t[:], bank[4][:, 0:KH * NX].rearrange("p (k e) -> p e k", e=NX)).then_inc(b1_ready, 1)

        @block.scalar
        def _(act):
            def normalise(b, q, n_rows):
                act.wait_ge(coef_ready, b + 1)
                for j, n in enumerate(n_rows):
                    last = nc.scalar.activation(rows[q][0:n, j, :], rows[q][0:n, j, :], ACT.Identity,
                                                bias=shift[q][0:n, j:j + 1], scale=rstd[q][0:n, j:j + 1])
                last.then_inc(norm_done, 1)

            with act.Fori(0, NLB // LBUF) as i:
                for q in range(LBUF):
                    normalise(i * LBUF + q, q, [P] * LB)
            normalise(NLB, 0, tail_rows)


def plan_after_sums(sums_done):
    plan = []
    for k, (t0, t1) in enumerate(PARTS):
        pairs = (t1 - t0) // 2
        plan += [(1, [("ready", sums_done, k)]), (pairs, [("linear", t0 // 2, k)]), (1, [("coefficients", 0, k)]),
                 (pairs, [("norm", t0 // 2, k)]), (1, [("route", 0, k)]),
                 (pairs, [("send", t0 // 2, k)]), (1, [("first_items", 0, k)])]
        beside = ITEMS[k] // 2 - 1
        if k:
            s0, s1 = PARTS[k - 1]
            both = min(beside, (s1 - s0) // 2)
            assert both == (s1 - s0) // 2
            plan += [(both, [("items", FIRST[k] // 2, k), ("combine", s0 // 2, k - 1)]),
                     (beside - both, [("items", FIRST[k] // 2 + both, k)])]
        else:
            plan += [(beside, [("items", 0, k)])]
        plan += [(1, [("last_items", 0, k)])]
    t0, t1 = PARTS[-1]
    plan += [((t1 - t0) // 2, [("combine", t0 // 2, len(PARTS) - 1)])]
    return plan


PLAN_GENERAL = plan_after_sums(0)
PLAN = [(NG // 2, [("sums", 0, 0)])] + plan_after_sums(NG)


def run(eng, plan, steps):
    for turns, work in plan:
        mine = [(steps[kind], first, part, kind) for kind, first, part in work if kind in steps]
        if not mine or not turns:
            continue
        first = int(turns == 1 or any(f == 0 for _, f, _, _ in mine))
        last = int(turns > first and any(kind in ("linear", "send", "combine") and f + turns == NT // 2
                                         for _, f, _, kind in mine))
        for r in range(first):
            for step, f, part, _ in mine:
                step(f + r, part)
        if turns - last > first:
            with eng.Fori(first, turns - last) as r:
                for step, f, part, _ in mine:
                    step(r + f, part)
        for r in range(turns - last, turns) if last else ():
            for step, f, part, _ in mine:
                step(f + r, part)


def layers(nc, m, x, xhat, w1, b1_cols, w2, b2, slots_x, slots_y, out):
    acc, bank, ident = m["acc"], m["bank"], m["ident"]
    B_SUM, B_TURN, B_XI, B_H, B_Y, B_NODE, B_GATE = bank[0], bank[1], bank[2], bank[3:5], bank[5], bank[6], bank[7]
    with ExitStack() as s:
        sb = lambda name, shape, dt=F32: s.enter_context(nc.sbuf_tensor(name, shape, dt))
        ring = lambda name, shape, dt=F32: [sb(f"{name}{i}", shape, dt) for i in range(2)]
        sem = lambda name: s.enter_context(nc.semaphore(name))
        sems = lambda name: [sem(f"{name}{i}") for i in range(2)]
        rows, index = ring("rows", [P, CG, D]), ring("index", [P, CG], I32)
        in_win, spread = ring("in_win", [P, CG]), ring("spread", [P, CG, W])
        sums_n = sb("sums_n", [W, D])
        win_start = sb("win_start", [1, NG + 1], I32)
        x_t, sums_t = ring("x_t", [P, D]), ring("sums_t", [P, KD, P])
        bn6, mv2, mv = ring("bn6", [P, 6]), sb("mv2", [P, 2, 2]), sb("mv", [P, NT, 2])
        std, rstd, shift = sb("std", [P, NT]), sb("rstd", [P, NT]), sb("shift", [P, NT])
        xn = sb("xn", [P, 2, D])
        xnT = sb("xnT", [P, 2, KD, P])
        RW = [P, NTM, NX]
        prob, mask1, mask2, cand, both = (sb(n, RW) for n in ("prob", "mask1", "mask2", "cand", "both"))
        pos, count_et, upto_et = sb("pos", RW), sb("count_et", [P, NX, NTM]), sb("upto_et", [P, NX, NTM])
        keep_et = sb("keep_et", [P, NX, NTM])
        top, top_r = sb("top", [P, NTM]), sb("top_r", [P, NTM])
        weight = sb("weight", [P, NT, 2])
        slot_f, slot_i = sb("slot_f", [P, NTM, 2]), sb("slot_i", [P, NT, 2], I32)
        rev = sb("rev", [P, NX])
        below, ones = sb("below", [P, P]), sb("ones", [P, P])
        valid, part_iota = sb("valid", [P, 1]), sb("part_iota", [P, 1])
        cnt_i, items_i = sb("cnt_i", [P, NX], I32), sb("items_i", [P, NX], I32)
        items_f, upto_f, first_f = sb("items_f", [P, NX]), sb("upto_f", [P, NX]), sb("first_f", [P, NX])
        item_iota = sb("item_iota", [1, max(ITEMS)])
        item_f, item_e = ring("item_f", [1, max(ITEMS)]), sb("item_e", [1, NI + 2], I32)
        send, send_i = [xn[:, q, :] for q in range(2)], ring("send_i", [P, 2], I32)
        got, got_i, res = ring("got", [P, 2, D]), ring("got_i", [P, 2], I32), ring("res", [P, D])
        xi, xiT = ring("xi", [P, TB, D]), ring("xiT", [P, KD, IT])
        w1_i, w2_i = ring("w1_i", [P, KD, H]), ring("w2_i", [P, KH, D])
        b1_i, b2_i = ring("b1_i", [P, KH]), ring("b2_i", [P, D])
        hT, y_i = ring("hT", [P, KH, IT]), ring("y_i", [P, TB, D])
        zeros = y_i[0][:].rearrange("p b f -> p (b f)")
        wins_f, wsum_f, ones_row = w1_i[0][0:1, 0, 0:NG], w1_i[0][0:1, 1, 0:NG], w1_i[1][0:1, 0, 0:NG]

        set0, set1, route_step, zeros_set, zeroed = sem("set0"), sem("set1"), sem("route_step"), sem("zeros_set"), sem("zeroed")
        index_ready, rows_begun, rows_in = sem("index_ready"), sem("rows_begun"), sems("rows_in")
        in_win_ready, spread_ready, summed = sem("in_win_ready"), sem("spread_ready"), sem("summed")
        sums_n_ready, sums_turned, added = sem("sums_n_ready"), sem("sums_turned"), sem("added")
        win_ready, win_spread, win_summed, win_added, win_rows = (
            sem("win_ready"), sem("win_spread"), sem("win_summed"), sem("win_added"), sems("win_rows"))
        x_in, x_biased, sums_out, lin_summed, lin_added = sems("x_in"), sem("x_biased"), sem("sums_out"), sem("lin_summed"), sem("lin_added")
        lin_stats, lin_seen, lin_aggr, lin_kept, node_read = sem("lin_stats"), sem("lin_seen"), sem("lin_aggr"), sem("lin_kept"), sem("node_read")
        win_table, win_group, part_ready = sem("win_table"), sem("win_group"), sem("part_ready")
        lin_done, std_ready, coef_ready = sem("lin_done"), sem("std_ready"), sem("coef_ready")
        xn_ready, xn_turned, xnT_ready, logits_done, gate_read = sem("xn_ready"), sem("xn_turned"), sem("xnT_ready"), sem("logits_done"), sem("gate_read")
        exp_ready, exp_done, mask_ready, ranked, routed = sem("exp_ready"), sem("exp_done"), sem("mask_ready"), sem("ranked"), sem("routed")
        send_ready, send_idx, send_begun, sent = sem("send_ready"), sem("send_idx"), sem("send_begun"), sems("sent")
        got_idx, got_begun, got_in, got_half, res_ready, res_out = sem("got_idx"), sem("got_begun"), sems("got_in"), sem("got_half"), sem("res_ready"), sems("res_out")
        xi_in, w1_in, w2_in = sems("xi_in"), sems("w1_in"), sems("w2_in")
        xi_turned, xiT_ready, h_summed, h_ready, y_summed, y_ready, y_out = (
            sem("xi_turned"), sem("xiT_ready"), sem("h_summed"), sem("h_ready"), sem("y_summed"), sem("y_ready"), sems("y_out"))
        block = s.enter_context(nc.Block())

        def tile(t):
            return acc[:, :, bass.ds(t * P, P)]

        by_block = lambda a: a.rearrange("p (k j) -> p k j", k=KD)
        gathers = 16 * CG

        def either(eng, steps, general):
            wide = eng.value_load(m["wide"][:], min_val=0, max_val=1)
            with eng.If(wide == 0):
                run(eng, PLAN, steps)
            with eng.Else():
                general()
                run(eng, PLAN_GENERAL, steps)

        @block.gpsimd
        def _(pool):
            nc.gpsimd.memset(zeros, 0.0).then_inc(zeros_set, 1)
            nc.gpsimd.memset(ones[:], 1.0)
            nc.gpsimd.memset(ones_row, 1.0)
            nc.gpsimd.memset(win_start[:, 0:1], 0)
            for q in range(2):
                nc.gpsimd.memset(x_t[q][:], 0.0)
                nc.gpsimd.memset(got[q][:], 0.0)
            nc.gpsimd.memset(keep_et[:], 1.0).then_inc(set0, 1)
            pool.wait_ge(set0, 1)
            pool.affine_select(out=below[:], in_=ones[:], compare_op=ALU.is_gt, fill=0.0, base=0,
                               pattern=[[1, P]], channel_multiplier=-1)
            nc.gpsimd.memset(keep_et[:, :, 0:1], 0.0)
            nc.gpsimd.iota(rev[:], pattern=[[-1, NX]], base=NX, channel_multiplier=0,
                           allow_small_or_imprecise_dtypes=True)
            nc.gpsimd.iota(part_iota[:], pattern=[[0, 1]], base=0, channel_multiplier=1,
                           allow_small_or_imprecise_dtypes=True)
            nc.gpsimd.iota(item_iota[:], pattern=[[1, max(ITEMS)]], base=0, channel_multiplier=0,
                           allow_small_or_imprecise_dtypes=True).then_inc(set1, 1)

            def gather_group(q, done):
                for c in range(CG):
                    pool.indirect_dma_start(
                        rows[q][:, c, :], None, xhat,
                        bass.IndirectOffsetOnAxis(ap=index[q][:, c:c + 1], axis=0)).then_inc(done, 16)

            def sums(v, part):
                for q in range(2):
                    pool.wait_ge(index_ready, v * 2 + q + 1)
                    pool.sem_inc(rows_begun, 1)
                    gather_group(q, rows_in[q])

            def send_tiles(u, part):
                for q in range(2):
                    t = u * 2 + q
                    n = LAST if isinstance(t, int) and t == NT - 1 else P
                    pool.wait_ge(zeroed, NI * 16)
                    pool.wait_ge(send_idx, t + 1)
                    pool.sem_inc(send_begun, 1)
                    for k in range(2):
                        pool.indirect_dma_start(slots_x[part], bass.IndirectOffsetOnAxis(ap=send_i[q][0:n, k:k + 1], axis=0),
                                                send[q][0:n, :], None).then_inc(sent[q], 16)

            def combine(u, part):
                for q in range(2):
                    pool.wait_ge(y_out[q], FIRST[part + 1] // 2 * 16)
                for q in range(2):
                    t = u * 2 + q
                    n = LAST if isinstance(t, int) and t == NT - 1 else P
                    pool.wait_ge(got_idx, t + 1)
                    pool.sem_inc(got_begun, 1)
                    for k in range(2):
                        pool.indirect_dma_start(got[q][0:n, k, :], None, slots_y[part],
                                                bass.IndirectOffsetOnAxis(ap=got_i[q][0:n, k:k + 1], axis=0)).then_inc(got_in[q], 16)

            def general():
                with pool.Fori(0, NG // 2) as v:
                    for q in range(2):
                        pool.wait_ge(index_ready, v * 2 + q + 1)
                        pool.sem_inc(rows_begun, 1)
                        gather_group(q, win_rows[q])

            either(pool, {"sums": sums, "send": send_tiles, "combine": combine}, general)

        @block.sync
        def _(sp):
            sp.wait_ge(zeros_set, 1)
            for k in range(len(PARTS)):
                tiled = slots_x[k].rearrange("(n p j) f -> n p (j f)", p=P, j=2)
                with sp.Fori(0, ITEMS[k]) as i:
                    sp.dma_start(tiled[bass.ds(i, 1)].rearrange("o p f -> p (o f)"), zeros).then_inc(zeroed, 16)
            sp.wait_ge(set0, 1)

            def linear(u, part):
                for q in range(2):
                    t = u * 2 + q
                    sp.wait_ge(lin_added, t + 1)
                    if isinstance(t, int) and t == NT - 1:
                        sp.dma_start(x_t[q][0:LAST, :], x[t * P:N, :]).then_inc(x_in[q], 16)
                    else:
                        sp.dma_start(x_t[q][:], x[bass.ds(t * P, P), :]).then_inc(x_in[q], 16)

            def expert(i):
                return sp.value_load(item_e[:, bass.ds(i, 1)], min_val=0, max_val=NX - 1)

            def load_xi(i, q, part):
                rows_of = slots_x[part][bass.ds((i - FIRST[part]) * IT, IT), :].rearrange("(b p) f -> p b f", p=P)
                sp.dma_start(xi[q][:], rows_of).then_inc(xi_in[q], 16)

            def load_w1(e, q):
                sp.dma_start(w1_i[q][:], w1[bass.ds(e, 1)].rearrange("o (b p) h -> p (o b) h", p=P)).then_inc(w1_in[q], 16)
                sp.dma_start(b1_i[q][:], b1_cols[bass.ds(e, 1)].rearrange("o p k -> p (o k)")).then_inc(w1_in[q], 16)

            def load_w2(e, q):
                sp.dma_start(w2_i[q][:], w2[bass.ds(e, 1)].rearrange("o (b p) f -> p (o b) f", p=P)).then_inc(w2_in[q], 16)
                sp.dma_start(b2_i[q][:], b2[bass.ds(e, 1)].rearrange("o f -> (o f)").partition_broadcast(P)).then_inc(w2_in[q], 16)

            def store_results(i, q, part):
                sp.wait_ge(y_ready, i + 3)
                rows_of = slots_y[part][bass.ds((i - FIRST[part]) * IT, IT), :].rearrange("(b p) f -> p b f", p=P)
                sp.dma_start(rows_of, y_i[q][:]).then_inc(y_out[q], 16)

            def first_items(_, part):
                sp.wait_ge(routed, part + 1)
                for q in range(2):
                    sp.wait_ge(sent[q], PARTS[part][1] // 2 * 32)
                for q in range(2):
                    load_xi(FIRST[part] + q, q, part)
                    e = expert(FIRST[part] + q)
                    load_w1(e, q)
                    load_w2(e, q)

            def items(v, part):
                for q in range(2):
                    i = v * 2 + q
                    sp.wait_ge(xi_turned, i + 1)
                    load_xi(i + 2, q, part)
                    e = expert(i + 2)
                    sp.wait_ge(h_ready, i * KH + 3 * KH)
                    load_w1(e, q)
                    store_results(i, q, part)
                    load_w2(e, q)

            def last_items(_, part):
                for q in range(2):
                    store_results(FIRST[part + 1] - 2 + q, q, part)

            def combine(u, part):
                for q in range(2):
                    t = u * 2 + q
                    sp.wait_ge(res_ready, t + 3)
                    if isinstance(t, int) and t == NT - 1:
                        sp.dma_start(out[t * P:N, :], res[q][0:LAST, :]).then_inc(res_out[q], 16)
                    else:
                        sp.dma_start(out[bass.ds(t * P, P), :], res[q][:]).then_inc(res_out[q], 16)

            either(sp, {"linear": linear, "first_items": first_items, "items": items, "last_items": last_items,
                        "combine": combine}, lambda: None)
            for q in range(2):
                sp.wait_ge(res_out[q], NT // 2 * 16)

        @block.tensor
        def _(pe):
            pe.sem_inc(summed, 2)
            pe.sem_inc(sums_turned, 1)
            pe.sem_inc(lin_summed, 2)
            pe.sem_inc(xn_turned, 1)
            pe.sem_inc(logits_done, 1)
            pe.sem_inc(h_summed, 2 * KH)
            pe.sem_inc(y_summed, 2)
            pe.wait_ge(set1, 1)

            def turn_sums(g):
                pe.wait_ge(sums_n_ready, g + 2)
                pe.wait_ge(added, g + 1)
                for k in range(KD):
                    last = nc.tensor.transpose(B_TURN[:, k * W:(k + 1) * W], sums_n[:, k * P:(k + 1) * P], ident[0:W, 0:W])
                last.then_inc(sums_turned, 1)

            def sums(v, part):
                for q in range(2):
                    g = v * 2 + q
                    pe.wait_ge(spread_ready, g + 1)
                    pe.wait_ge(sums_n_ready, g + 1)
                    pe.wait_ge(rows_in[q], v * gathers + gathers)
                    for c in range(CG):
                        last = nc.tensor.matmul(B_SUM[0:W, 0:D], spread[q][:, c, :], rows[q][:, c, :],
                                                start=c == 0, stop=c == CG - 1)
                    last.then_inc(summed, 1)
                    turn_sums(g)

            def linear(u, part):
                pe.wait_ge(node_read, u + PARTS[part][0] // 2 + 1)
                for q in range(2):
                    pe.wait_ge(sums_out, u * 2 + q + 1)
                    for k in range(KD):
                        last = nc.tensor.matmul(B_NODE[:, q * D:(q + 1) * D], sums_t[q][:, k, :], m["gnn_wT"][:, k, :],
                                                start=k == 0, stop=k == KD - 1)
                    last.then_inc(lin_summed, 1)

            def norm(u, part):
                pe.wait_ge(xn_ready, u + 1)
                pe.wait_ge(node_read, u + PARTS[part][1] // 2 + 1)
                for q in range(2):
                    for k in range(KD):
                        last = nc.tensor.transpose(B_NODE[:, (q * KD + k) * P:(q * KD + k + 1) * P],
                                                   xn[:, q, k * P:(k + 1) * P], ident[:])
                last.then_inc(xn_turned, 1)
                pe.wait_ge(xnT_ready, u + 1)
                pe.wait_ge(gate_read, u + part + 1)
                for q in range(2):
                    for k in range(KD):
                        last = nc.tensor.matmul(B_GATE[:, q * NX:(q + 1) * NX], xnT[:, q, k, :], m["gate_wS"][:, k, :],
                                                start=k == 0, stop=k == KD - 1)
                last.then_inc(logits_done, 1)

            def route(_, part):
                t0, t1 = PARTS[part]
                n = (t1 - t0) * NX
                pe.wait_ge(mask_ready, part + 1)
                chosen = both[:, 0:t1 - t0, :].rearrange("p t e -> p (t e)")
                nc.tensor.matmul(B_GATE[:, 0:n], below[:], chosen, start=True, stop=True)
                nc.tensor.matmul(B_GATE[:, n:2 * n], ones[:], chosen, start=True, stop=True).then_inc(ranked, 1)

            def turn(i, q):
                pe.wait_ge(xi_in[q], i * 8 - 8 * q + 16)
                pe.wait_ge(xiT_ready, i + 2)
                for k in range(KD):
                    for b in range(TB):
                        last = nc.tensor.transpose(B_XI[:, k * IT + b * P:k * IT + (b + 1) * P],
                                                   xi[q][:, b, k * P:(k + 1) * P], ident[:])
                last.then_inc(xi_turned, 1)

            def up(i, q):
                pe.wait_ge(xiT_ready, i + 3)
                pe.wait_ge(w1_in[q], i * 16 - 16 * q + 32)
                for j in range(KH):
                    if j % 2 == 0:
                        pe.wait_ge(h_ready, i * KH + KH + j + 2)
                    for k in range(KD):
                        last = nc.tensor.matmul(B_H[j // 2][:, j % 2 * IT:(j % 2 + 1) * IT],
                                                w1_i[q][:, k, j * P:(j + 1) * P], xiT[q][:, k, :],
                                                start=k == 0, stop=k == KD - 1)
                    last.then_inc(h_summed, 1)

            def down(i, q):
                pe.wait_ge(h_ready, i * KH + 3 * KH)
                pe.wait_ge(w2_in[q], i * 16 - 16 * q + 32)
                pe.wait_ge(y_ready, i + 2)
                for b in range(TB):
                    for j in range(KH):
                        last = nc.tensor.matmul(B_Y[:, b * D:(b + 1) * D], hT[q][:, j, b * P:(b + 1) * P],
                                                w2_i[q][:, j, :], start=j == 0, stop=j == KH - 1)
                last.then_inc(y_summed, 1)

            def first_items(_, part):
                i = FIRST[part]
                turn(i, 0)
                turn(i + 1, 1)
                up(i, 0)

            def items(v, part):
                for q in range(2):
                    i = v * 2 + q
                    up(i + 1, 1 - q)
                    turn(i + 2, q)
                    down(i, q)

            def last_items(_, part):
                i = FIRST[part + 1] - 2
                up(i + 1, 1)
                down(i, 0)
                down(i + 1, 1)

            def general():
                pe.wait_ge(win_table, 1)
                with pe.Fori(0, NG // 2) as v:
                    for q in range(2):
                        w0 = pe.value_load(win_start[:, bass.ds(v * 2 + q, 1)], min_val=0, max_val=MAX_WINDOWS)
                        w1 = pe.value_load(win_start[:, bass.ds(v * 2 + q + 1, 1)], min_val=1, max_val=MAX_WINDOWS)
                        with pe.Fori(w0, w1) as w:
                            pe.wait_ge(win_rows[q], v * gathers + gathers)
                            pe.wait_ge(win_spread, w + 1)
                            pe.wait_ge(win_added, w + 1)
                            for k in range(KD):
                                for c in range(CG):
                                    last = nc.tensor.matmul(B_SUM[:, k * WG:(k + 1) * WG], rows[q][:, c, k * P:(k + 1) * P],
                                                            spread[0][:, c, 0:WG], start=c == 0, stop=c == CG - 1)
                            last.then_inc(win_summed, 1)

            either(pe, {"sums": sums, "linear": linear, "norm": norm, "route": route,
                        "first_items": first_items, "items": items, "last_items": last_items}, general)

        @block.scalar
        def _(act):
            act.sem_inc(sums_n_ready, 1)
            act.sem_inc(h_ready, 2 * KH)
            act.wait_ge(set1, 1)

            def sources(g, q):
                act.wait_ge(summed, g + 1)
                nc.scalar.activation(index[q][:], m["src_t"][:, bass.ds(g * CG, CG)], ACT.Copy).then_inc(index_ready, 1)

            def sums(v, part):
                for q in range(2):
                    g = v * 2 + q
                    if isinstance(g, int) and g < 2:
                        if g == 0:
                            sources(0, 0)
                            sources(1, 1)
                    act.wait_ge(summed, g + 3)
                    act.wait_ge(sums_turned, g + 1)
                    nc.scalar.activation(sums_n[:], B_SUM[0:W, 0:D], ACT.Copy).then_inc(sums_n_ready, 1)
                    sources(g + 2, q)

            def linear(u, part):
                act.wait_ge(part_ready, part + 1)
                for q in range(2):
                    t = u * 2 + q
                    act.wait_ge(lin_summed, t + 1)
                    nc.scalar.activation(sums_t[q][:], tile(t), ACT.Copy).then_inc(sums_out, 1)

            def coefficients(_, part):
                t0, t1 = PARTS[part]
                act.wait_ge(lin_done, part + 1)
                nc.scalar.activation(std[:, t0:t1], mv[:, t0:t1, 1], ACT.Sqrt, bias=m["eps"][:]).then_inc(std_ready, 1)
                act.wait_ge(coef_ready, part + 1)

            def normalised(to, t):
                col = bass.ds(t, 1)
                return nc.scalar.activation(to, tile(t), ACT.Identity, bias=shift[:, col], scale=rstd[:, col])

            def norm(u, part):
                act.wait_ge(xn_turned, u + 1)
                for q in range(2):
                    last = normalised(by_block(xn[:, q, :]), u * 2 + q)
                last.then_inc(xn_ready, 1)

            def route(_, part):
                t0, t1 = PARTS[part]
                act.wait_ge(exp_ready, part + 1)
                nc.scalar.activation(prob[:, 0:t1 - t0, :], prob[:, 0:t1 - t0, :], ACT.Exp).then_inc(exp_done, 1)
                act.wait_ge(routed, part + 1)

            def send_tiles(u, part):
                for q in range(2):
                    t = u * 2 + q
                    if not isinstance(u, int) or u > 0:
                        act.wait_ge(sent[q], u * 32)
                    normalised(by_block(send[q]), t).then_inc(send_ready, 1)
                    nc.scalar.activation(send_i[q][:], slot_i[:, bass.ds(t, 1), :].rearrange("p o k -> p (o k)"),
                                         ACT.Copy).then_inc(send_idx, 1)

            def gelu(i, q):
                act.wait_ge(y_summed, i + 1)
                act.wait_ge(w1_in[q], i * 16 - 16 * q + 32)
                for j in range(KH):
                    if j % 2 == 0:
                        act.wait_ge(h_summed, i * KH + 2 * KH + j + 2)
                    nc.scalar.activation(hT[q][:, j, :], B_H[j // 2][:, j % 2 * IT:(j % 2 + 1) * IT],
                                         ACT.Gelu, bias=b1_i[q][:, j:j + 1]).then_inc(h_ready, 1)

            def first_items(_, part):
                gelu(FIRST[part], 0)

            def items(v, part):
                for q in range(2):
                    gelu(v * 2 + q + 1, 1 - q)

            def last_items(_, part):
                gelu(FIRST[part + 1] - 1, 1)

            def combine(u, part):
                for q in range(2):
                    t = u * 2 + q
                    act.wait_ge(res_ready, t + 1)
                    nc.scalar.activation(got_i[q][:], slot_i[:, bass.ds(t, 1), :].rearrange("p o k -> p (o k)"),
                                         ACT.Copy).then_inc(got_idx, 1)

            def general():
                with act.Fori(0, NG // 2) as v:
                    for q in range(2):
                        act.wait_ge(win_group, v * 2 + q + 1)
                        nc.scalar.activation(index[q][:], m["src_t"][:, bass.ds((v * 2 + q) * CG, CG)],
                                             ACT.Copy).then_inc(index_ready, 1)

            either(act, {"sums": sums, "linear": linear, "coefficients": coefficients, "norm": norm, "route": route,
                         "send": send_tiles, "first_items": first_items, "items": items, "last_items": last_items,
                         "combine": combine}, general)

        @block.vector
        def _(dve):
            dve.sem_inc(in_win_ready, 1)
            dve.sem_inc(added, 1)
            dve.sem_inc(win_added, 1)
            dve.sem_inc(win_ready, 1)
            dve.sem_inc(win_group, 2)
            dve.sem_inc(lin_added, 2)
            dve.sem_inc(node_read, 1)
            dve.sem_inc(gate_read, 1)
            dve.sem_inc(xiT_ready, 2)
            dve.sem_inc(y_ready, 2)
            dve.sem_inc(res_ready, 2)
            dve.wait_ge(set1, 1)
            nc.vector.tensor_scalar(valid[:], part_iota[:], float(LAST), None, op0=ALU.is_lt)

            def spread_group(g, q):
                dve.wait_ge(summed, g + 1)
                nc.vector.tensor_copy(in_win[q][:], m["dst_rel"][:, bass.ds(g * CG, CG)]).then_inc(in_win_ready, 1)
                dve.wait_ge(in_win_ready, g + 2)
                for c in range(CG):
                    last = nc.vector.tensor_scalar(spread[q][:, c, :], m["iota_w"][:], in_win[q][:, c:c + 1],
                                                   m["wgt"][:, bass.ds(g * CG + c, 1)], op0=ALU.is_equal, op1=ALU.mult)
                last.then_inc(spread_ready, 1)

            def add_group(g):
                base = dve.value_load(m["base_i"][:, bass.ds(g, 1)], min_val=0, max_val=N - 1)
                here = acc[:, :, bass.ds(base, W)]
                dve.wait_ge(sums_turned, g + 2)
                dve.wait_ge(added, g + 1)
                nc.vector.tensor_tensor(here, here, B_TURN[:, 0:KD * W].rearrange("p (k w) -> p k w", k=KD),
                                        op=ALU.add).then_inc(added, 1)

            def sums(v, part):
                for q in range(2):
                    g = v * 2 + q
                    if isinstance(g, int) and g == 0:
                        spread_group(0, 0)
                    spread_group(g + 1, 1 - q)
                    add_group(g)

            def linear(u, part):
                for q in range(2):
                    t = u * 2 + q
                    dve.wait_ge(x_in[q], u * 16 + 16)
                    nc.vector.tensor_tensor(x_t[q][:], x_t[q][:], m["gnn_bB"][:], op=ALU.add).then_inc(x_biased, 1)
                for q in range(2):
                    t = u * 2 + q
                    dve.wait_ge(x_biased, t + 1)
                    dve.wait_ge(lin_summed, u * 2 + 4)
                    nc.vector.tensor_tensor(tile(t), by_block(B_NODE[:, q * D:(q + 1) * D]), by_block(x_t[q][:]),
                                            op=ALU.add).then_inc(lin_added, 1)
                dve.wait_ge(lin_added, u * 2 + 4)
                dve.sem_inc(node_read, 1)
                for q in range(2):
                    t = u * 2 + q
                    dve.sem_inc(lin_seen, 1)
                    nc.vector.bn_stats(bn6[q][:], tile(t)).then_inc(lin_stats, 1)
                for q in range(2):
                    t = u * 2 + q
                    dve.wait_ge(lin_stats, t + 1)
                    dve.sem_inc(lin_seen, 1)
                    last = nc.vector.bn_aggr(mv2[:, q, :], bn6[q][:])
                last.then_inc(lin_aggr, 1)
                dve.wait_ge(lin_aggr, u + 1)
                nc.vector.tensor_copy(mv[:, bass.ds(u * 2, 2), :], mv2[:]).then_inc(lin_kept, 1)

            def coefficients(_, part):
                t0, t1 = PARTS[part]
                dve.wait_ge(lin_kept, t1 // 2)
                dve.sem_inc(lin_done, 1)
                dve.wait_ge(std_ready, part + 1)
                then(nc.vector.reciprocal(rstd[:, t0:t1], std[:, t0:t1]))
                nc.vector.scalar_tensor_tensor(shift[:, t0:t1], mv[:, t0:t1, 0], -1.0, rstd[:, t0:t1],
                                               op0=ALU.mult, op1=ALU.mult).then_inc(coef_ready, 1)

            def norm(u, part):
                dve.wait_ge(xn_turned, u + 2)
                dve.wait_ge(logits_done, u + 1)
                nc.vector.tensor_copy(xnT[:].rearrange("p q k j -> p (q k j)"), B_NODE[:]).then_inc(xnT_ready, 1)
                dve.wait_ge(xnT_ready, u + 1)
                dve.sem_inc(node_read, 1)
                dve.wait_ge(logits_done, u + 2)
                nc.vector.tensor_tensor(prob[:, bass.ds(u * 2 - PARTS[part][0], 2), :],
                                        B_GATE[:, 0:2 * NX].rearrange("p (q e) -> p q e", q=2),
                                        m["gate_bB"][:].unsqueeze(1).to_broadcast([P, 2, NX]),
                                        op=ALU.add).then_inc(gate_read, 1)

            steps = [0]

            def then(instruction):
                instruction.then_inc(route_step, 1)
                steps[0] += 1
                dve.wait_ge(route_step, steps[0])

            def route(_, part):
                t0, t1 = PARTS[part]
                n = t1 - t0
                pr, m1, m2, cd, bo, ps = (a[:, 0:n, :] for a in (prob, mask1, mask2, cand, both, pos))
                per_tile = lambda a: a[:, 0:n].unsqueeze(2).to_broadcast([P, n, NX])
                per_expert = lambda a: a[:].unsqueeze(1).to_broadcast([P, n, NX])
                dve.wait_ge(gate_read, t1 // 2 + part + 1)
                then(nc.vector.tensor_reduce(top[:, 0:n], pr, axis=AX.X, op=ALU.max))
                nc.vector.tensor_tensor(pr, pr, per_tile(top), op=ALU.subtract).then_inc(exp_ready, 1)
                dve.wait_ge(exp_done, part + 1)
                then(nc.vector.tensor_reduce(top[:, 0:n], pr, axis=AX.X, op=ALU.add))
                then(nc.vector.reciprocal(top_r[:, 0:n], top[:, 0:n]))
                then(nc.vector.tensor_tensor(pr, pr, per_tile(top_r), op=ALU.mult))
                for k, mk in enumerate((m1, m2)):
                    then(nc.vector.tensor_reduce(weight[:, t0:t1, k], pr, axis=AX.X, op=ALU.max))
                    then(nc.vector.tensor_tensor(cd, pr, weight[:, t0:t1, k:k + 1].to_broadcast([P, n, NX]), op=ALU.is_equal))
                    then(nc.vector.tensor_tensor(cd, cd, per_expert(rev), op=ALU.mult))
                    then(nc.vector.tensor_reduce(top[:, 0:n], cd, axis=AX.X, op=ALU.max))
                    then(nc.vector.tensor_tensor(mk, cd, per_tile(top), op=ALU.is_equal))
                    if k == 0:
                        then(nc.vector.scalar_tensor_tensor(pr, m1, -2.0, pr, op0=ALU.mult, op1=ALU.add))
                if t1 == NT:
                    for mk in (m1, m2):
                        then(nc.vector.tensor_scalar(mk[:, n - 1, :], mk[:, n - 1, :], valid[:], None, op0=ALU.mult))
                nc.vector.tensor_tensor(bo, m1, m2, op=ALU.add).then_inc(mask_ready, 1)
                dve.wait_ge(ranked, part + 1)
                counts = count_et[:, :, 0:n]
                upto = upto_et[:, :, 0:n]
                flat = lambda a: a[:].rearrange("p e t -> p (e t)")
                then(nc.vector.tensor_copy(counts, B_GATE[:, n * NX:2 * n * NX].rearrange("p (t e) -> p e t", e=NX)))
                if n < NTM:
                    then(nc.vector.memset(count_et[:, :, n:], 0.0))
                then(nc.vector.tensor_tensor_scan(flat(upto_et), flat(keep_et), flat(count_et), 0.0, op0=ALU.mult, op1=ALU.add))
                total = upto_et[:, :, n - 1]
                then(nc.vector.tensor_scalar(cnt_i[:], total, float(IT - 1), None, op0=ALU.add))
                then(nc.vector.tensor_scalar(items_i[:], cnt_i[:], IT.bit_length() - 1, None, op0=ALU.arith_shift_right))
                then(nc.vector.tensor_copy(items_f[:], items_i[:]))
                then(nc.vector.tensor_tensor_scan(upto_f[:], ones[:, 0:NX], items_f[:], 0.0, op0=ALU.mult, op1=ALU.add))
                then(nc.vector.tensor_tensor(first_f[:], upto_f[:], items_f[:], op=ALU.subtract))
                then(nc.vector.tensor_scalar(first_f[:], first_f[:], float(IT), None, op0=ALU.mult))
                then(nc.vector.tensor_tensor(upto, upto, counts, op=ALU.subtract))
                then(nc.vector.tensor_tensor(ps, upto.rearrange("p e t -> p t e"), per_expert(first_f), op=ALU.add))
                then(nc.vector.tensor_tensor(ps, ps, B_GATE[:, 0:n * NX].rearrange("p (t e) -> p t e", e=NX), op=ALU.add))
                dve.sem_inc(gate_read, 1)
                for k, mk in enumerate((m1, m2)):
                    then(nc.vector.tensor_tensor(cd, mk, ps, op=ALU.mult))
                    then(nc.vector.tensor_reduce(slot_f[:, 0:n, k], cd, axis=AX.X, op=ALU.add))
                then(nc.vector.tensor_copy(slot_i[:, t0:t1, :], slot_f[:, 0:n, :]))
                ni, i0 = ITEMS[part], FIRST[part]
                then(nc.vector.tensor_scalar(item_f[1][:, 0:ni], item_iota[:, 0:ni], upto_f[0:1, 0:1], None, op0=ALU.is_ge))
                for e in range(1, NX - 1):
                    then(nc.vector.scalar_tensor_tensor(item_f[1 - e % 2][:, 0:ni], item_iota[:, 0:ni], upto_f[0:1, e:e + 1],
                                                        item_f[e % 2][:, 0:ni], op0=ALU.is_ge, op1=ALU.add))
                then(nc.vector.tensor_copy(item_e[:, i0:i0 + ni], item_f[1 - (NX - 2) % 2][:, 0:ni]))
                dve.sem_inc(routed, 1)

            def turned_items(i, q):
                dve.wait_ge(xi_turned, i + 1)
                dve.wait_ge(h_summed, i * KH + KH)
                nc.vector.tensor_copy(xiT[q][:].rearrange("p k j -> p (k j)"), B_XI[:]).then_inc(xiT_ready, 1)

            def results(i, q):
                dve.wait_ge(w2_in[q], i * 16 - 16 * q + 32)
                if not isinstance(i, int) or i > 1:
                    dve.wait_ge(y_out[q], i * 8 - 8 * q)
                dve.wait_ge(y_summed, i + 3)
                nc.vector.tensor_tensor(y_i[q][:], B_Y[:].rearrange("p (b f) -> p b f", b=TB),
                                        b2_i[q][:].unsqueeze(1).to_broadcast([P, TB, D]), op=ALU.add).then_inc(y_ready, 1)

            def first_items(_, part):
                for q in range(2):
                    turned_items(FIRST[part] + q, q)

            def items(v, part):
                for q in range(2):
                    turned_items(v * 2 + q + 2, q)
                    results(v * 2 + q, q)

            def last_items(_, part):
                for q in range(2):
                    results(FIRST[part + 1] - 2 + q, q)

            def combine(u, part):
                for q in range(2):
                    t = u * 2 + q
                    dve.wait_ge(got_in[q], u * 32 + 32)
                    nc.vector.scalar_tensor_tensor(by_block(got[q][:, 0, :]), by_block(got[q][:, 0, :]),
                                                   weight[:, bass.ds(t, 1), 0:1].rearrange("p o k -> p (o k)"),
                                                   tile(t), op0=ALU.mult, op1=ALU.add).then_inc(got_half, 1)
                for q in range(2):
                    t = u * 2 + q
                    dve.wait_ge(got_half, t + 1)
                    if not isinstance(u, int) or u > 0:
                        dve.wait_ge(res_out[q], u * 16)
                    nc.vector.scalar_tensor_tensor(res[q][:], got[q][:, 1, :],
                                                   weight[:, bass.ds(t, 1), 1:2].rearrange("p o k -> p (o k)"),
                                                   got[q][:, 0, :], op0=ALU.mult, op1=ALU.add).then_inc(res_ready, 1)

            def ready(sums_done, part):
                if sums_done:
                    dve.wait_ge(added, sums_done + 1)
                dve.sem_inc(part_ready, 1)

            def general():
                steps[0] = 0
                then(nc.vector.tensor_scalar(m["last_rel"][:], m["last_rel"][:], WG.bit_length() - 1, None, op0=ALU.arith_shift_right))
                then(nc.vector.tensor_scalar(wins_f, m["last_rel"][:], 1.0, None, op0=ALU.add))
                then(nc.vector.tensor_tensor_scan(wsum_f, ones_row, wins_f, 0.0, op0=ALU.mult, op1=ALU.add))
                then(nc.vector.tensor_copy(win_start[:, 1:NG + 1], wsum_f))
                dve.sem_inc(win_table, 1)
                with dve.Fori(0, NG // 2) as v:
                    for q in range(2):
                        g = v * 2 + q
                        w0 = dve.value_load(win_start[:, bass.ds(g, 1)], min_val=0, max_val=MAX_WINDOWS)
                        w1 = dve.value_load(win_start[:, bass.ds(g + 1, 1)], min_val=1, max_val=MAX_WINDOWS)
                        base = dve.value_load(m["base_i"][:, bass.ds(g, 1)], min_val=0, max_val=N - 1)
                        dve.wait_ge(win_ready, w0 + g + 1)
                        nc.vector.tensor_copy(in_win[0][:], m["dst_rel"][:, bass.ds(g * CG, CG)]).then_inc(win_ready, 1)
                        with dve.Fori(w0, w1) as w:
                            dve.wait_ge(win_ready, w + g + 2)
                            for c in range(CG):
                                last = nc.vector.tensor_scalar(spread[0][:, c, 0:WG], m["iota_w"][:, 0:WG], in_win[0][:, c:c + 1],
                                                               m["wgt"][:, bass.ds(g * CG + c, 1)],
                                                               op0=ALU.is_equal, op1=ALU.mult)
                            last.then_inc(win_spread, 1)
                            dve.wait_ge(win_spread, w + 1)
                            nc.vector.tensor_scalar(in_win[0][:], in_win[0][:], float(WG), None, op0=ALU.subtract).then_inc(win_ready, 1)
                            dve.wait_ge(win_summed, w + 1)
                            dve.wait_ge(win_added, w + 1)
                            at = nc.s_assert_within(base + (w - w0) * WG, 0, NPAD,
                                                    skip_runtime_bounds_check_because="the window holds a node below N")
                            here = acc[:, :, bass.ds(at, WG)]
                            nc.vector.tensor_tensor(here, here, B_SUM[:, 0:KD * WG].rearrange("p (k w) -> p k w", k=KD),
                                                    op=ALU.add).then_inc(win_added, 1)
                        dve.sem_inc(win_group, 1)
                windows = dve.value_load(win_start[:, NG:NG + 1], min_val=1, max_val=MAX_WINDOWS)
                dve.wait_ge(win_added, windows + 1)
                dve.sem_inc(win_group, 1)

            either(dve, {"sums": sums, "ready": ready, "linear": linear, "coefficients": coefficients, "norm": norm,
                         "route": route, "first_items": first_items, "items": items, "last_items": last_items,
                         "combine": combine}, general)


_INS = ["x", "src", "dst", "edge_weight", "L0_gnn_W", "L0_gnn_b", "L0_ffn_gate_w", "L0_ffn_gate_b",
        "L0_ffn_W1", "L0_ffn_b1", "L0_ffn_W2", "L0_ffn_b2"]


def kernel(**inputs):
    import numpy as np
    import concourse.bacc as bacc
    from concourse.bass_utils import run_bass_kernel_spmd

    nc = bacc.Bacc("TRN2", target_bir_lowering=False, num_devices=1)
    arrays, args = {}, []
    for name in _INS:
        a = np.ascontiguousarray(inputs[name])
        arrays["in_" + name] = a
        args.append(nc.dram_tensor("in_" + name, a.shape, mybir.dt.from_np(a.dtype), kind="ExternalInput").ap())
    out = nc.dram_tensor("out_nodes", (N, D), F32, kind="ExternalOutput").ap()
    build(nc, *args, out)
    return run_bass_kernel_spmd(nc, [arrays], core_ids=[0]).results[0]["out_nodes"]
```

```python
from contextlib import ExitStack

import concourse.bass as bass
from concourse import mybir

F32 = mybir.dt.float32
I32 = mybir.dt.int32
U16 = mybir.dt.uint16
ALU = mybir.AluOpType
ACT = mybir.ActivationFunctionType
AX = mybir.AxisListType

P = 128
N, D = 12500, 256
E_EDGES = 212500
NX, H = 8, 512
KD = D // P
KH = H // P
EPS = 1e-5

CG = 8
GROUP = CG * P
NG = -(-E_EDGES // GROUP)
NG += NG % 2
NCH = NG * CG
FULL_CHUNKS = E_EDGES // P
REST_EDGES = E_EDGES - FULL_CHUNKS * P
CB = NCH // P
CB_FULL = FULL_CHUNKS // P
assert CB * P == NCH and CB_FULL == CB - 1
LAST_ROWS = FULL_CHUNKS - CB_FULL * P
W = 80
WG = 64
MAX_WINDOWS = NG + N // WG + 1

NT = -(-N // P)
LAST = N - (NT - 1) * P
NPAD = NT * P

LB = 8
LJ = N // P
NLB = LJ // LB
LREST = N - LJ * P
LBUF = 4
assert LJ == NLB * LB + 1 and NLB % LBUF == 0

IT = 256
TB = IT // P

PARTS = ((0, 16), (16, 40), (40, 64), (64, 84), (84, NT))
assert all(t0 % 4 == 0 for t0, _ in PARTS)
NTM = max(t1 - t0 for t0, t1 in PARTS)


def n_items(t0, t1):
    pairs = 2 * (min(t1 * P, N) - t0 * P)
    n = (pairs + NX * (IT - 1)) // IT
    return n + n % 2


ITEMS = [n_items(*p) for p in PARTS]
FIRST = [sum(ITEMS[:k]) for k in range(len(PARTS) + 1)]
NI = FIRST[-1]
PAIRS = {"linear": 4, "norm": 4, "send": 2, "fetch": 1}
READY = [min(NG, -(-t1 * P * E_EDGES // (N * GROUP)) + 4 & ~1) for _, t1 in PARTS[:-1]] + [NG]


def build(nc, x, src, dst, edge_weight, gnn_w, gnn_b, gate_w, gate_b, w1, b1, w2, b2, out):
    xhat = nc.dram_tensor("xhat", (N, D), F32, kind="Internal").ap()
    slots_x = [nc.dram_tensor(f"slots_x{k}", (n * IT, D), F32, kind="Internal").ap() for k, n in enumerate(ITEMS)]
    slots_y = [nc.dram_tensor(f"slots_y{k}", (n * IT, D), F32, kind="Internal").ap() for k, n in enumerate(ITEMS)]
    b1_cols = nc.dram_tensor("b1_cols", (NX, P, KH), F32, kind="Internal").ap()
    with ExitStack() as mem:
        sb = lambda name, shape, dt=F32: mem.enter_context(nc.sbuf_tensor(name, shape, dt))
        m = {
            "acc": sb("acc", [P, KD, NPAD + W]),
            "ident": sb("ident", [P, P]),
            "gnn_wT": sb("gnn_wT", [P, KD, D]),
            "gate_wS": sb("gate_wS", [P, KD, NX]),
            "gate_bB": sb("gate_bB", [P, NX]),
            "gnn_bB": sb("gnn_bB", [P, D]),
            "eps": sb("eps", [P, 1]),
            "dst_rel": sb("dst_rel", [P, NCH + 2 * CG], U16),
            "src_t": sb("src_t", [P, NCH + 2 * CG], U16),
            "wgt": sb("wgt", [P, NCH + 2 * CG]),
            "win_start": sb("win_start", [1, NG + 1], I32),
            "base_i": sb("base_i", [1, NG], I32),
            "wide": sb("wide", [1, 1], I32),
            "iota_w": sb("iota_w", [P, W]),
            "bank": [mem.enter_context(nc.psum_tensor(f"bank{i}", [P, 512], F32)) for i in range(8)],
        }
        prepare(nc, m, x, src, dst, edge_weight, gnn_w, gnn_b, gate_w, gate_b, b1, b1_cols, xhat)
        layers(nc, m, x, xhat, w1, b1_cols, w2, b2, slots_x, slots_y, out)


def prepare(nc, m, x, src, dst, edge_weight, gnn_w, gnn_b, gate_w, gate_b, b1, b1_cols, xhat):
    ident, bank = m["ident"], m["bank"]
    with ExitStack() as s:
        sb = lambda name, shape, dt=F32: s.enter_context(nc.sbuf_tensor("pre_" + name, shape, dt))
        sem = lambda name: s.enter_context(nc.semaphore("pre_" + name))
        dst_raw = sb("dst_raw", [P, CB, P], I32)
        src_raw = sb("src_raw", [P, CB, P], I32)
        wgt_raw = sb("wgt_raw", [P, CB, P])
        dst_f, src_f = sb("dst_f", [P, CB, P]), sb("src_f", [P, CB, P])
        base_b = sb("base_b", [P, NG])
        last_i = sb("last_i", [1, NG], I32)
        base_f, span_f, span_max, wide_f = sb("base_f", [1, NG]), sb("span_f", [1, NG]), sb("span_max", [1, 1]), sb("wide_f", [1, 1])
        flags = sb("flags", [1, len(PARTS)])
        last_rel, wins_i, wins_f = sb("last_rel", [1, NG], I32), sb("wins_i", [1, NG], I32), sb("wins_f", [1, NG])
        wsum_f, ones_ng = sb("wsum_f", [1, NG]), sb("ones_ng", [1, NG])
        ones_row = sb("ones_row", [1, P])
        gnn_raw = sb("gnn_raw", [P, KD, D])
        b1_raw = sb("b1_raw", [NX, H])
        b1_t = sb("b1_t", [P, NX, KH])
        rows = [sb(f"rows{i}", [P, LB, D]) for i in range(LBUF)]
        stats = [sb(f"stats{i}", [P, LB, 6]) for i in range(2)]
        mv = [sb(f"mv{i}", [P, LB, 2]) for i in range(LBUF)]
        var_eps, rstd = ([sb(f"{n}{i}", [P, LB]) for i in range(LBUF)] for n in ("var_eps", "rstd"))
        mean_rstd, shift = ([sb(f"{n}{i}", [P, LB]) for i in range(LBUF)] for n in ("mean_rstd", "shift"))
        eps8, half8, minus8 = sb("eps8", [P, LB]), sb("half8", [P, LB]), sb("minus8", [P, LB])
        pad_set, zero_set, ident_set, consts = sem("pad_set"), sem("zero_set"), sem("ident_set"), sem("consts")
        edges_in, base_in, params_in = sem("edges_in"), sem("base_in"), sem("params_in")
        as_float, turned, turned_out, params_turned = sem("as_float"), sem("turned"), sem("turned_out"), sem("params_turned")
        win_step = sem("win_step")
        dve_step, b1_ready, b1_stored = sem("dve_step"), sem("b1_ready"), sem("b1_stored")
        loaded = [sem(f"loaded{i}") for i in range(LBUF)]
        stored = [sem(f"stored{i}") for i in range(LBUF)]
        stats_done, stats_seen, mv_ready = sem("stats_done"), sem("stats_seen"), sem("mv_ready")
        base_spread, base_b_set = sem("base_spread"), sem("base_b_set")
        pow_step, coef_ready, norm_done = sem("pow_step"), sem("coef_ready"), sem("norm_done")

        x_main = x[0:P * LJ].rearrange("(p j) f -> p j f", p=P)
        h_main = xhat[0:P * LJ].rearrange("(p j) f -> p j f", p=P)
        turns = [(k, b, min(4, CB - b)) for k in range(3) for b in range(0, CB, 4)]
        tail_rows = (P, LREST)
        block = s.enter_context(nc.Block())

        @block.gpsimd
        def _(pool):
            nc.gpsimd.memset(dst_raw[:, CB - 1, :], 40000)
            nc.gpsimd.memset(src_raw[:, CB - 1, :], 0)
            nc.gpsimd.memset(wgt_raw[:, CB - 1, :], 0.0).then_inc(pad_set, 1)
            nc.gpsimd.memset(ident[:], 0.0).then_inc(zero_set, 1)
            nc.gpsimd.memset(eps8[:], EPS)
            nc.gpsimd.memset(half8[:], -0.5)
            nc.gpsimd.memset(minus8[:], -1.0)
            nc.gpsimd.memset(ones_row[:], 1.0)
            nc.gpsimd.memset(ones_ng[:], 1.0)
            pool.wait_ge(zero_set, 1)
            pool.affine_select(out=ident[:], in_=ident[:], compare_op=ALU.not_equal, fill=1.0, base=0,
                               pattern=[[-1, P]], channel_multiplier=1).then_inc(ident_set, 1)
            nc.gpsimd.iota(m["iota_w"][:], pattern=[[1, W]], base=0, channel_multiplier=0,
                           allow_small_or_imprecise_dtypes=True)
            nc.gpsimd.memset(m["src_t"][:, NCH:], 0)
            nc.gpsimd.memset(m["dst_rel"][:, NCH:], 0)
            nc.gpsimd.memset(m["wgt"][:, NCH:], 0.0)
            nc.gpsimd.memset(m["eps"][:], EPS).then_inc(consts, 1)
            pool.wait_ge(consts, 1)

            def coefficients(b, q):
                pool.wait_ge(mv_ready, b + 3)
                nc.gpsimd.tensor_tensor(var_eps[q][:], mv[q][:, :, 1], eps8[:], op=ALU.add).then_inc(pow_step, 1)
                pool.wait_ge(pow_step, b * 3 + 1)
                nc.gpsimd.tensor_tensor(rstd[q][:], var_eps[q][:], half8[:], op=ALU.pow).then_inc(pow_step, 1)
                pool.wait_ge(pow_step, b * 3 + 2)
                nc.gpsimd.tensor_tensor(mean_rstd[q][:], mv[q][:, :, 0], rstd[q][:], op=ALU.mult).then_inc(pow_step, 1)
                pool.wait_ge(pow_step, b * 3 + 3)
                nc.gpsimd.tensor_tensor(shift[q][:], mean_rstd[q][:], minus8[:], op=ALU.mult).then_inc(coef_ready, 1)

            with pool.Fori(0, NLB // LBUF) as i:
                for q in range(LBUF):
                    coefficients(i * LBUF + q, q)
            coefficients(NLB, 0)
            nc.gpsimd.memset(m["acc"][:], 0.0).then_inc(consts, 1)

        @block.sync
        def _(sp):
            full = CB_FULL * P * P
            arrays = ((dst_raw, dst), (src_raw, src), (wgt_raw, edge_weight))
            dst_row = dst.rearrange("(o n) -> o n", o=1)

            def load(b):
                sp.dma_start(rows[b % LBUF][:], x_main[:, b * LB:(b + 1) * LB, :]).then_inc(loaded[b % LBUF], 16)

            load(0)
            load(1)
            for raw, e in arrays:
                sp.dma_start(raw[:, 0:CB_FULL, :],
                             e[0:full].rearrange("(b p e) -> p b e", p=P, e=P)).then_inc(edges_in, 16)
            sp.wait_ge(pad_set, 1)
            for raw, e in arrays:
                body = e[full:FULL_CHUNKS * P].rearrange("(p e) -> p e", e=P)
                sp.dma_start(raw[0:LAST_ROWS, CB - 1, :], body).then_inc(edges_in, 16)
                rest = e[FULL_CHUNKS * P:E_EDGES].rearrange("(p e) -> p e", p=1)
                sp.dma_start(raw[LAST_ROWS:LAST_ROWS + 1, CB - 1, 0:REST_EDGES], rest).then_inc(edges_in, 16)
            sp.dma_start(m["base_i"][:], dst_row[:, 0:E_EDGES:GROUP], allow_slow_non_contiguous=True).then_inc(base_in, 16)
            sp.dma_start(last_i[:, 0:NG - 1], dst_row[:, GROUP - 1:E_EDGES:GROUP],
                         allow_slow_non_contiguous=True).then_inc(base_in, 16)
            sp.dma_start(last_i[:, NG - 1:NG], dst_row[:, E_EDGES - 1:E_EDGES]).then_inc(base_in, 16)
            load(2)
            for to, a in ((gnn_raw[:], gnn_w.rearrange("(b p) i -> p b i", p=P)), (b1_raw[:], b1),
                          (m["gate_wS"][:], gate_w.rearrange("(b p) e -> p b e", p=P)),
                          (m["gate_bB"][:], gate_b.partition_broadcast(P)),
                          (m["gnn_bB"][:], gnn_b.partition_broadcast(P))):
                sp.dma_start(to, a).then_inc(params_in, 16)
            for b in range(NLB):
                q = b % LBUF
                sp.wait_ge(norm_done, b + 1)
                sp.dma_start(h_main[:, b * LB:(b + 1) * LB, :], rows[q][:]).then_inc(stored[q], 16)
                nxt = b + LBUF - 1
                if nxt >= LBUF and nxt <= NLB:
                    sp.wait_ge(stored[nxt % LBUF], nxt // LBUF * 16)
                if nxt < NLB:
                    load(nxt)
                elif nxt == NLB:
                    sp.dma_start(rows[0][:, 0, :], x_main[:, LJ - 1, :]).then_inc(loaded[0], 16)
                    sp.dma_start(rows[0][0:LREST, 1, :], x[P * LJ:N]).then_inc(loaded[0], 16)
            sp.wait_ge(norm_done, NLB + 1)
            sp.dma_start(h_main[:, LJ - 1, :], rows[0][:, 0, :]).then_inc(stored[0], 16)
            sp.dma_start(xhat[P * LJ:N], rows[0][0:LREST, 1, :]).then_inc(stored[0], 16)
            sp.wait_ge(b1_ready, 1)
            sp.dma_start(b1_cols.rearrange("e p k -> p e k"), b1_t[:]).then_inc(b1_stored, 16)
            for q in range(LBUF):
                sp.wait_ge(stored[q], (NLB // LBUF + 2 * (q == 0)) * 16)
            sp.wait_ge(params_in, 5 * 16)
            sp.wait_ge(b1_stored, 16)

        @block.tensor
        def _(pe):
            pe.wait_ge(ident_set, 1)
            pe.wait_ge(as_float, 3)
            pe.wait_ge(consts, 1)
            nc.tensor.matmul(bank[2][:, 0:NG], ones_row[:], base_f[:], start=True, stop=True).then_inc(base_spread, 1)
            for t, (k, b0, nb) in enumerate(turns):
                raw = (dst_f, src_f, wgt_raw)[k]
                if t >= 2:
                    pe.wait_ge(turned_out, t - 1)
                for j in range(nb):
                    last = nc.tensor.transpose(bank[t % 2][:, j * P:(j + 1) * P], raw[:, b0 + j, :], ident[:])
                last.then_inc(turned, 1)
            pe.wait_ge(params_in, 5 * 16)
            for ib in range(KD):
                for ob in range(KD):
                    last = nc.tensor.transpose(bank[3][:, (ib * KD + ob) * P:(ib * KD + ob + 1) * P],
                                               gnn_raw[:, ob, ib * P:(ib + 1) * P], ident[:])
            for hb in range(KH):
                last = nc.tensor.transpose(bank[4][:, hb * NX:(hb + 1) * NX],
                                           b1_raw[:, hb * P:(hb + 1) * P], ident[0:NX, 0:NX])
            last.then_inc(params_turned, 1)

        @block.vector
        def _(dve):
            dve.sem_inc(mv_ready, 2)
            dve.wait_ge(edges_in, 9 * 16)
            nc.vector.tensor_copy(dst_f[:], dst_raw[:]).then_inc(as_float, 1)
            nc.vector.tensor_copy(src_f[:], src_raw[:]).then_inc(as_float, 1)
            dve.wait_ge(base_in, 3 * 16)
            nc.vector.tensor_copy(base_f[:], m["base_i"][:]).then_inc(as_float, 1)
            nc.vector.tensor_tensor(last_rel[:], last_i[:], m["base_i"][:], op=ALU.subtract).then_inc(dve_step, 1)
            nc.vector.tensor_tensor(span_f[:], last_i[:], m["base_i"][:], op=ALU.subtract).then_inc(dve_step, 1)
            dve.wait_ge(dve_step, 2)
            dve.wait_ge(as_float, 3)
            nc.vector.tensor_reduce(span_max[:], span_f[:], axis=AX.X, op=ALU.max).then_inc(dve_step, 1)
            dve.wait_ge(dve_step, 3)
            nc.vector.tensor_scalar(flags[:, 0:1], span_max[:], float(W), None, op0=ALU.is_ge).then_inc(dve_step, 1)
            for k in range(len(PARTS) - 1):
                nc.vector.tensor_scalar(flags[:, k + 1:k + 2], base_f[:, READY[k]:READY[k] + 1], float(PARTS[k][1] * P),
                                        None, op0=ALU.is_lt).then_inc(dve_step, 1)
            dve.wait_ge(dve_step, 3 + len(PARTS))
            nc.vector.tensor_reduce(wide_f[:], flags[:], axis=AX.X, op=ALU.max).then_inc(dve_step, 1)
            dve.wait_ge(dve_step, 4 + len(PARTS))
            nc.vector.tensor_copy(m["wide"][:], wide_f[:])
            nc.vector.memset(m["win_start"][:, 0:1], 0)
            nc.vector.tensor_scalar(wins_i[:], last_rel[:], WG.bit_length() - 1, None,
                                    op0=ALU.arith_shift_right).then_inc(win_step, 1)
            dve.wait_ge(win_step, 1)
            nc.vector.tensor_scalar(wins_f[:], wins_i[:], 1.0, None, op0=ALU.add).then_inc(win_step, 1)
            dve.wait_ge(win_step, 2)
            dve.wait_ge(consts, 1)
            nc.vector.tensor_tensor_scan(wsum_f[:], ones_ng[:], wins_f[:], 0.0, op0=ALU.mult, op1=ALU.add).then_inc(win_step, 1)
            dve.wait_ge(win_step, 3)
            nc.vector.tensor_copy(m["win_start"][:, 1:NG + 1], wsum_f[:])
            dve.wait_ge(base_spread, 1)
            nc.vector.tensor_copy(base_b[:], bank[2][:, 0:NG]).then_inc(base_b_set, 1)
            dve.wait_ge(base_b_set, 1)
            for t, (k, b0, nb) in enumerate(turns):
                dve.wait_ge(turned, t + 1)
                cols = slice(b0 * P, (b0 + nb) * P)
                if k == 0:
                    g0 = b0 * P // CG
                    ng = nb * P // CG
                    nc.vector.tensor_tensor(m["dst_rel"][:, cols].rearrange("p (g c) -> p g c", c=CG),
                                            bank[t % 2][:, 0:nb * P].rearrange("p (g c) -> p g c", c=CG),
                                            base_b[:, g0:g0 + ng].unsqueeze(2).to_broadcast([P, ng, CG]),
                                            op=ALU.subtract).then_inc(turned_out, 1)
                elif k == 1:
                    nc.vector.tensor_copy(m["src_t"][:, cols], bank[t % 2][:, 0:nb * P]).then_inc(turned_out, 1)
                else:
                    nc.vector.tensor_copy(m["wgt"][:, cols], bank[t % 2][:, 0:nb * P]).then_inc(turned_out, 1)

            def moments(b, q, n_rows):
                dve.wait_ge(mv_ready, b + 1)
                for j, n in enumerate(n_rows):
                    last = nc.vector.bn_stats(stats[q % 2][0:n, j, :], rows[q][0:n, j, :])
                last.then_inc(stats_done, 1)
                dve.wait_ge(stats_done, b + 1)
                dve.sem_inc(stats_seen, 1)
                for j, n in enumerate(n_rows):
                    last = nc.vector.bn_aggr(mv[q][0:n, j, :], stats[q % 2][0:n, j, :])
                last.then_inc(mv_ready, 1)

            with dve.Fori(0, NLB // LBUF) as i:
                for q in range(LBUF):
                    dve.wait_ge(loaded[q], i * 16 + 16)
                    moments(i * LBUF + q, q, [P] * LB)
            nc.vector.memset(mv[0][:], 1.0).then_inc(dve_step, 1)
            dve.wait_ge(dve_step, 5 + len(PARTS))
            dve.wait_ge(loaded[0], (NLB // LBUF + 2) * 16)
            moments(NLB, 0, tail_rows)
            dve.wait_ge(params_turned, 1)
            nc.vector.tensor_copy(m["gnn_wT"][:].rearrange("p b o -> p (b o)"), bank[3][:])
            nc.vector.tensor_copy(b1_t[:], bank[4][:, 0:KH * NX].rearrange("p (k e) -> p e k", e=NX)).then_inc(b1_ready, 1)

        @block.scalar
        def _(act):
            def normalise(b, q, n_rows):
                act.wait_ge(coef_ready, b + 1)
                for j, n in enumerate(n_rows):
                    last = nc.scalar.activation(rows[q][0:n, j, :], rows[q][0:n, j, :], ACT.Identity,
                                                bias=shift[q][0:n, j:j + 1], scale=rstd[q][0:n, j:j + 1])
                last.then_inc(norm_done, 1)

            with act.Fori(0, NLB // LBUF) as i:
                for q in range(LBUF):
                    normalise(i * LBUF + q, q, [P] * LB)
            normalise(NLB, 0, tail_rows)


def plan(with_sums):
    turns = []
    sums = list(range(NG // 2)) if with_sums else []
    ready_after = [g // 2 if with_sums else 0 for g in READY]
    nodes, items, combined = [], [], []
    for k, (t0, t1) in enumerate(PARTS):
        pairs = range(t0 // 2, t1 // 2)
        some = lambda kind: [(kind, pairs[j:j + PAIRS[kind]], k) for j in range(0, len(pairs), PAIRS[kind])]
        nodes += [("ready", [ready_after[k]], k)] + some("linear") + [("coefficients", range(2), k)] + some("norm")
        nodes += [("route", range(2), k), ("route", range(2, 4), k)] + some("send")
        items += [("first_items", [0], k)] + [("items", [i], k) for i in range(FIRST[k] // 2, FIRST[k + 1] // 2 - 1)]
        items += [("last_items", [0], k)]
        combined += some("fetch")
    sent, done, summed, turn_no = -1, {}, 0, 0
    while sums or nodes or items or combined:
        work, sent_now = [], sent
        if combined and combined[0][2] in done and turn_no > done[combined[0][2]] + 2 and (
                not sums or items and items[0][2] <= sent):
            work.append(combined.pop(0))
        if nodes and nodes[0][0] == "send":
            work.append(nodes.pop(0))
            if not nodes or nodes[0][0] != "send":
                sent_now = work[-1][2]
        if sums:
            work.append(("sums", [sums.pop(0)], 0))
        if nodes and nodes[0][0] != "send" and (nodes[0][0] != "ready" or nodes[0][1][0] <= summed) and "send" not in [w[0] for w in work]:
            work.append(nodes.pop(0))
        if items and items[0][2] <= sent:
            work.append(items.pop(0))
            if work[-1][0] == "last_items":
                done[work[-1][2]] = turn_no
        work += [("combine", w[1], w[2]) for w in work if w[0] == "fetch"]
        sent = sent_now
        turn_no += 1
        summed += "sums" in [w[0] for w in work]
        if not work:
            continue
        if turns:
            n, first = turns[-1]
            if len(first) == len(work) and all(
                    a[0] == b[0] and a[3] == b[2] and a[2] == len(b[1]) and a[0] in LOOPED and a[1] + n * a[2] == b[1][0]
                    for a, b in zip(first, work)):
                turns[-1] = (n + 1, first)
                continue
        turns.append((1, [(kind, at[0], len(at), part) for kind, at, part in work]))
    return turns


HALVES = ("sums", "items")
EARLY = ("send", "fetch")
PAIR_RINGS = ("linear", "send")
LOOPED = ("sums", "linear", "norm", "send", "items", "fetch", "combine")
PLAN, PLAN_GENERAL = plan(True), plan(False)


def run(eng, plan, steps, gathers_first=False):
    def turn(work, r):
        lanes = {"early": [], "halves": [], "nodes": []}
        for kind, f, m, part in work:
            for j in range(m):
                lane = "early" if kind in EARLY else "halves" if kind in HALVES else "nodes"
                for q in range(2) if kind in HALVES else (None,):
                    lanes[lane].append((kind, r * m + (f + j), part, (f + j) % 2 if kind in PAIR_RINGS else q))
                    assert kind not in PAIR_RINGS or isinstance(r, int) or m % 2 == 0
        halves, early = lanes["halves"], lanes["early"]
        nodes = [n for n in lanes["nodes"] if n[0] != "combine"]
        combine = [n for n in lanes["nodes"] if n[0] == "combine"]
        order = halves[:2] + early if gathers_first else early + halves[:1] + nodes[:1] + halves[1:2] + combine + nodes[1:2]
        for j in range(2, max(len(halves), len(nodes))):
            order += halves[j:j + 1] + nodes[j:j + 1]
        for kind, u, part, q in order:
            if kind in steps:
                steps[kind](*((u, part) if q is None else (u, part, q)))

    for turns, work in plan:
        if not any(kind in steps for kind, _, _, _ in work):
            continue
        first = int(turns == 1 or any(f == 0 for _, f, _, _ in work))
        last = int(turns > first and any(kind not in HALVES and f + turns * m >= NT // 2 - (kind == "linear")
                                         for kind, f, m, _ in work))
        if first:
            turn(work, 0)
        if turns - last > first:
            with eng.Fori(first, turns - last) as r:
                turn(work, r)
        if last:
            turn(work, turns - 1)


def layers(nc, m, x, xhat, w1, b1_cols, w2, b2, slots_x, slots_y, out):
    acc, bank, ident = m["acc"], m["bank"], m["ident"]
    B_SUM, B_TURN, B_XI, B_H, B_Y, B_NODE, B_GATE = bank[0], bank[1], bank[2], bank[3:5], bank[5], bank[6], bank[7]
    with ExitStack() as s:
        sb = lambda name, shape, dt=F32: s.enter_context(nc.sbuf_tensor(name, shape, dt))
        ring = lambda name, shape, dt=F32: [sb(f"{name}{i}", shape, dt) for i in range(2)]
        sem = lambda name: s.enter_context(nc.semaphore(name))
        sems = lambda name: [sem(f"{name}{i}") for i in range(2)]
        rows, index = ring("rows", [P, CG, D]), ring("index", [P, CG], I32)
        in_win, spread = ring("in_win", [P, CG]), ring("spread", [P, CG, W])
        sums_n = sb("sums_n", [W, D])
        win_start = m["win_start"]
        x_t, sums_t = ring("x_t", [P, D]), ring("sums_t", [P, KD, P])
        bn6, mv2, mv = ring("bn6", [P, 6]), sb("mv2", [P, 2, 2]), sb("mv", [P, NT, 2])
        std, rstd, shift = sb("std", [P, NT]), sb("rstd", [P, NT]), sb("shift", [P, NT])
        xn = sb("xn", [P, 2, D])
        xnT = sb("xnT", [P, 2, KD, P])
        RW = [P, NTM, NX]
        prob, mask1, mask2, cand, both = (sb(n, RW) for n in ("prob", "mask1", "mask2", "cand", "both"))
        pos, count_et, upto_et = sb("pos", RW), sb("count_et", [P, NX, NTM]), sb("upto_et", [P, NX, NTM])
        keep_et = sb("keep_et", [P, NX, NTM])
        top, top_r = sb("top", [P, NTM]), sb("top_r", [P, NTM])
        weight = sb("weight", [P, NT, 2])
        slot_f, slot_i = sb("slot_f", [P, NTM, 2]), sb("slot_i", [P, NT, 2], I32)
        rev = sb("rev", [P, NX])
        below, ones = sb("below", [P, P]), sb("ones", [P, P])
        valid, part_iota = sb("valid", [P, 1]), sb("part_iota", [P, 1])
        cnt_i, items_i = sb("cnt_i", [P, NX], I32), sb("items_i", [P, NX], I32)
        items_f, upto_f, first_f = sb("items_f", [P, NX]), sb("upto_f", [P, NX]), sb("first_f", [P, NX])
        item_iota = sb("item_iota", [1, max(ITEMS)])
        item_f, item_e = ring("item_f", [1, max(ITEMS)]), sb("item_e", [1, NI + 2], I32)
        send_i = [[sb(f"send_i{o}{q}", [P, 2], I32) for q in range(2)] for o in range(2)]
        x_t = [x_t, [xn[:, q, :] for q in range(2)]]
        send = [[xn[:, q, :] for q in range(2)], [xnT[:, q, :, :].rearrange("p k j -> p (k j)") for q in range(2)]]
        got, got_i, res = ring("got", [P, 2, D]), ring("got_i", [P, 2], I32), ring("res", [P, D])
        xi, xiT = ring("xi", [P, TB, D]), ring("xiT", [P, KD, IT])
        w1_i, w2_i = ring("w1_i", [P, KD, H]), ring("w2_i", [P, KH, D])
        b1_i, b2_i = ring("b1_i", [P, KH]), ring("b2_i", [P, D])
        hT, y_i = ring("hT", [P, KH, IT]), ring("y_i", [P, TB, D])
        zeros = y_i[0][:].rearrange("p b f -> p (b f)")

        set0, set1, route_step, zeros_set, zeroed = sem("set0"), sem("set1"), sem("route_step"), sem("zeros_set"), sem("zeroed")
        index_ready, rows_begun, rows_in = sem("index_ready"), sem("rows_begun"), sems("rows_in")
        in_win_ready, spread_ready, summed = sem("in_win_ready"), sem("spread_ready"), sem("summed")
        sums_n_ready, sums_turned, added = sem("sums_n_ready"), sem("sums_turned"), sem("added")
        win_ready, win_spread, win_summed, win_added, win_rows = (
            sem("win_ready"), sem("win_spread"), sem("win_summed"), sem("win_added"), sems("win_rows"))
        x_in, x_biased, sums_out, lin_summed, lin_added = (sems("x_in_even"), sems("x_in_odd")), sem("x_biased"), sem("sums_out"), sem("lin_summed"), sem("lin_added")
        lin_stats, lin_seen, lin_aggr, lin_kept, node_read = sem("lin_stats"), sem("lin_seen"), sem("lin_aggr"), sem("lin_kept"), sem("node_read")
        win_group, part_ready = sem("win_group"), sem("part_ready")
        lin_done, std_ready, coef_ready = sem("lin_done"), sem("std_ready"), sem("coef_ready")
        xn_ready, xn_turned, xnT_ready, logits_done, gate_read = sem("xn_ready"), sem("xn_turned"), sem("xnT_ready"), sem("logits_done"), sem("gate_read")
        exp_ready, exp_done, mask_ready, ranked, routed = sem("exp_ready"), sem("exp_done"), sem("mask_ready"), sem("ranked"), sem("routed")
        send_ready, send_idx, send_begun, sent = sem("send_ready"), sem("send_idx"), sem("send_begun"), (sems("sent_even"), sems("sent_odd"))
        got_idx, got_begun, got_in, got_half, res_ready, res_out = sem("got_idx"), sem("got_begun"), sems("got_in"), sem("got_half"), sem("res_ready"), sems("res_out")
        xi_in, w1_in, w2_in = sems("xi_in"), sems("w1_in"), sems("w2_in")
        xi_turned, xiT_ready, h_summed, h_ready, y_summed, y_ready, y_out = (
            sem("xi_turned"), sem("xiT_ready"), sem("h_summed"), sem("h_ready"), sem("y_summed"), sem("y_ready"), sems("y_out"))
        block = s.enter_context(nc.Block())

        def tile(t):
            return acc[:, :, bass.ds(t * P, P)]

        def wait_sent(eng, part):
            pairs = (PARTS[part][1] // 2 + 1) // 2, PARTS[part][1] // 4
            for odd in range(2):
                for q in range(2):
                    eng.wait_ge(sent[odd][q], pairs[odd] * 32)

        by_block = lambda a: a.rearrange("p (k j) -> p k j", k=KD)
        gathers = 16 * CG

        def either(eng, steps, general, gathers_first=False):
            wide = eng.value_load(m["wide"][:], min_val=0, max_val=1)
            with eng.If(wide == 0):
                run(eng, PLAN, steps, gathers_first)
            with eng.Else():
                general()
                run(eng, PLAN_GENERAL, steps, gathers_first)

        @block.gpsimd
        def _(pool):
            nc.gpsimd.memset(zeros, 0.0).then_inc(zeros_set, 1)
            nc.gpsimd.memset(ones[:], 1.0)
            for q in range(2):
                nc.gpsimd.memset(x_t[0][q][:], 0.0)
                nc.gpsimd.memset(got[q][:], 0.0)
            nc.gpsimd.memset(keep_et[:], 1.0).then_inc(set0, 1)
            pool.wait_ge(set0, 1)
            pool.affine_select(out=below[:], in_=ones[:], compare_op=ALU.is_gt, fill=0.0, base=0,
                               pattern=[[1, P]], channel_multiplier=-1)
            nc.gpsimd.memset(keep_et[:, :, 0:1], 0.0)
            nc.gpsimd.iota(rev[:], pattern=[[-1, NX]], base=NX, channel_multiplier=0,
                           allow_small_or_imprecise_dtypes=True)
            nc.gpsimd.iota(part_iota[:], pattern=[[0, 1]], base=0, channel_multiplier=1,
                           allow_small_or_imprecise_dtypes=True)
            nc.gpsimd.iota(item_iota[:], pattern=[[1, max(ITEMS)]], base=0, channel_multiplier=0,
                           allow_small_or_imprecise_dtypes=True).then_inc(set1, 1)

            def gather_group(q, done):
                for c in range(CG):
                    pool.indirect_dma_start(
                        rows[q][:, c, :], None, xhat,
                        bass.IndirectOffsetOnAxis(ap=index[q][:, c:c + 1], axis=0)).then_inc(done, 16)

            def sums(v, part, q):
                pool.wait_ge(index_ready, v * 2 + q + 1)
                pool.sem_inc(rows_begun, 1)
                gather_group(q, rows_in[q])

            def send_tiles(u, part, odd):
                for q in range(2):
                    t = u * 2 + q
                    n = LAST if isinstance(t, int) and t == NT - 1 else P
                    pool.wait_ge(zeroed, NI * 16)
                    pool.wait_ge(send_idx, t + 1)
                    pool.sem_inc(send_begun, 1)
                    for k in range(2):
                        pool.indirect_dma_start(slots_x[part], bass.IndirectOffsetOnAxis(ap=send_i[odd][q][0:n, k:k + 1], axis=0),
                                                send[odd][q][0:n, :], None).then_inc(sent[odd][q], 16)

            def fetch(u, part):
                for q in range(2):
                    pool.wait_ge(y_out[q], FIRST[part + 1] // 2 * 16)
                for q in range(2):
                    t = u * 2 + q
                    n = LAST if isinstance(t, int) and t == NT - 1 else P
                    pool.wait_ge(res_ready, t + 1)
                    pool.wait_ge(got_idx, t + 1)
                    pool.sem_inc(got_begun, 1)
                    for k in range(2):
                        pool.indirect_dma_start(got[q][0:n, k, :], None, slots_y[part],
                                                bass.IndirectOffsetOnAxis(ap=got_i[q][0:n, k:k + 1], axis=0)).then_inc(got_in[q], 16)

            def general():
                with pool.Fori(0, NG // 2) as v:
                    for q in range(2):
                        pool.wait_ge(index_ready, v * 2 + q + 1)
                        pool.sem_inc(rows_begun, 1)
                        gather_group(q, win_rows[q])

            either(pool, {"sums": sums, "send": send_tiles, "fetch": fetch}, general, gathers_first=True)

        @block.sync
        def _(sp):
            sp.wait_ge(zeros_set, 1)
            for k in range(len(PARTS)):
                tiled = slots_x[k].rearrange("(n p j) f -> n p (j f)", p=P, j=2)
                with sp.Fori(0, ITEMS[k]) as i:
                    sp.dma_start(tiled[bass.ds(i, 1)].rearrange("o p f -> p (o f)"), zeros).then_inc(zeroed, 16)
            sp.wait_ge(set0, 1)

            def expert(i):
                return sp.value_load(item_e[:, bass.ds(i, 1)], min_val=0, max_val=NX - 1)

            def load_w1(e, q):
                sp.dma_start(w1_i[q][:], w1[bass.ds(e, 1)].rearrange("o (b p) h -> p (o b) h", p=P)).then_inc(w1_in[q], 16)
                sp.dma_start(b1_i[q][:], b1_cols[bass.ds(e, 1)].rearrange("o p k -> p (o k)")).then_inc(w1_in[q], 16)

            def load_w2(e, q):
                sp.dma_start(w2_i[q][:], w2[bass.ds(e, 1)].rearrange("o (b p) f -> p (o b) f", p=P)).then_inc(w2_in[q], 16)
                sp.dma_start(b2_i[q][:], b2[bass.ds(e, 1)].rearrange("o f -> (o f)").partition_broadcast(P)).then_inc(w2_in[q], 16)

            def store_results(i, q, part):
                sp.wait_ge(y_ready, i + 3)
                rows_of = slots_y[part][bass.ds((i - FIRST[part]) * IT, IT), :].rearrange("(b p) f -> p b f", p=P)
                sp.dma_start(rows_of, y_i[q][:]).then_inc(y_out[q], 16)

            def first_items(_, part):
                sp.wait_ge(routed, part + 1)
                for q in range(2):
                    e = expert(FIRST[part] + q)
                    load_w1(e, q)
                    load_w2(e, q)

            experts_next = [None, None]

            def items(v, part, q):
                if q == 0:
                    for p in range(2):
                        experts_next[p] = expert(v * 2 + 2 + p)
                    for p in range(2):
                        sp.wait_ge(h_ready, (v * 2 + p) * KH + 3 * KH)
                        load_w1(experts_next[p], p)
                store_results(v * 2 + q, q, part)
                load_w2(experts_next[q], q)

            def last_items(_, part):
                for q in range(2):
                    store_results(FIRST[part + 1] - 2 + q, q, part)

            def combine(u, part):
                for q in range(2):
                    t = u * 2 + q
                    sp.wait_ge(res_ready, t + 3)
                    if isinstance(t, int) and t == NT - 1:
                        sp.dma_start(out[t * P:N, :], res[q][0:LAST, :]).then_inc(res_out[q], 16)
                    else:
                        sp.dma_start(out[bass.ds(t * P, P), :], res[q][:]).then_inc(res_out[q], 16)

            either(sp, {"first_items": first_items, "items": items, "last_items": last_items,
                        "combine": combine}, lambda: None)
            for q in range(2):
                sp.wait_ge(res_out[q], NT // 2 * 16)

        @block.tensor
        def _(pe):
            pe.sem_inc(summed, 2)
            pe.sem_inc(sums_turned, 1)
            pe.sem_inc(lin_summed, 2)
            pe.sem_inc(xn_turned, 1)
            pe.sem_inc(logits_done, 1)
            pe.sem_inc(h_summed, 2 * KH)
            pe.sem_inc(y_summed, 2)
            pe.wait_ge(set1, 1)

            def turn_sums(g):
                pe.wait_ge(sums_n_ready, g + 2)
                pe.wait_ge(added, g + 1)
                for k in range(KD):
                    last = nc.tensor.transpose(B_TURN[:, k * W:(k + 1) * W], sums_n[:, k * P:(k + 1) * P], ident[0:W, 0:W])
                last.then_inc(sums_turned, 1)

            def sums(v, part, q):
                g = v * 2 + q
                pe.wait_ge(spread_ready, g + 1)
                pe.wait_ge(sums_n_ready, g + 1)
                pe.wait_ge(rows_in[q], v * gathers + gathers)
                for c in range(CG):
                    last = nc.tensor.matmul(B_SUM[0:W, 0:D], spread[q][:, c, :], rows[q][:, c, :],
                                            start=c == 0, stop=c == CG - 1)
                last.then_inc(summed, 1)
                turn_sums(g)

            def linear(u, part, odd):
                pe.wait_ge(node_read, PARTS[part][0] // 2 + 1)
                pe.wait_ge(gate_read, PARTS[part][0] // 2 + part + 1)
                for q in range(2):
                    pe.wait_ge(sums_out, u * 2 + q + 1)
                    pe.wait_ge(lin_added, u * 2 + q + 1)
                    for k in range(KD):
                        last = nc.tensor.matmul((B_NODE, B_GATE)[q][:, 0:D], sums_t[q][:, k, :], m["gnn_wT"][:, k, :],
                                                start=k == 0, stop=k == KD - 1)
                    last.then_inc(lin_summed, 1)

            def norm(u, part):
                pe.wait_ge(xn_ready, u + 1)
                pe.wait_ge(lin_added, PARTS[part][1] + 2)
                pe.wait_ge(node_read, u + 1)
                for q in range(2):
                    for k in range(KD):
                        last = nc.tensor.transpose(B_NODE[:, (q * KD + k) * P:(q * KD + k + 1) * P],
                                                   xn[:, q, k * P:(k + 1) * P], ident[:])
                last.then_inc(xn_turned, 1)
                pe.wait_ge(xnT_ready, u + 1)
                pe.wait_ge(gate_read, u + part + 1)
                for q in range(2):
                    for k in range(KD):
                        last = nc.tensor.matmul(B_GATE[:, q * NX:(q + 1) * NX], xnT[:, q, k, :], m["gate_wS"][:, k, :],
                                                start=k == 0, stop=k == KD - 1)
                last.then_inc(logits_done, 1)

            def route(stage, part):
                if stage != 2:
                    return
                t0, t1 = PARTS[part]
                n = (t1 - t0) * NX
                pe.wait_ge(mask_ready, part + 1)
                chosen = both[:, 0:t1 - t0, :].rearrange("p t e -> p (t e)")
                nc.tensor.matmul(B_GATE[:, 0:n], below[:], chosen, start=True, stop=True)
                nc.tensor.matmul(B_GATE[:, n:2 * n], ones[:], chosen, start=True, stop=True).then_inc(ranked, 1)

            def turn(i, q):
                pe.wait_ge(xi_in[q], i * 8 - 8 * q + 16)
                pe.wait_ge(xiT_ready, i + 2)
                for k in range(KD):
                    for b in range(TB):
                        last = nc.tensor.transpose(B_XI[:, k * IT + b * P:k * IT + (b + 1) * P],
                                                   xi[q][:, b, k * P:(k + 1) * P], ident[:])
                last.then_inc(xi_turned, 1)

            def up(i, q):
                pe.wait_ge(xiT_ready, i + 3)
                pe.wait_ge(w1_in[q], i * 16 - 16 * q + 32)
                for j in range(KH):
                    if j % 2 == 0:
                        pe.wait_ge(h_ready, i * KH + KH + j + 2)
                    for k in range(KD):
                        last = nc.tensor.matmul(B_H[j // 2][:, j % 2 * IT:(j % 2 + 1) * IT],
                                                w1_i[q][:, k, j * P:(j + 1) * P], xiT[q][:, k, :],
                                                start=k == 0, stop=k == KD - 1)
                    last.then_inc(h_summed, 1)

            def down(i, q):
                pe.wait_ge(h_ready, i * KH + 3 * KH)
                pe.wait_ge(w2_in[q], i * 16 - 16 * q + 32)
                pe.wait_ge(y_ready, i + 2)
                for b in range(TB):
                    for j in range(KH):
                        last = nc.tensor.matmul(B_Y[:, b * D:(b + 1) * D], hT[q][:, j, b * P:(b + 1) * P],
                                                w2_i[q][:, j, :], start=j == 0, stop=j == KH - 1)
                last.then_inc(y_summed, 1)

            def first_items(_, part):
                i = FIRST[part]
                turn(i, 0)
                turn(i + 1, 1)
                up(i, 0)

            def items(v, part, q):
                i = v * 2 + q
                up(i + 1, 1 - q)
                turn(i + 2, q)
                down(i, q)

            def last_items(_, part):
                i = FIRST[part + 1] - 2
                up(i + 1, 1)
                down(i, 0)
                down(i + 1, 1)

            def general():
                with pe.Fori(0, NG // 2) as v:
                    for q in range(2):
                        w0 = pe.value_load(win_start[:, bass.ds(v * 2 + q, 1)], min_val=0, max_val=MAX_WINDOWS)
                        w1 = pe.value_load(win_start[:, bass.ds(v * 2 + q + 1, 1)], min_val=1, max_val=MAX_WINDOWS)
                        with pe.Fori(w0, w1) as w:
                            pe.wait_ge(win_rows[q], v * gathers + gathers)
                            pe.wait_ge(win_spread, w + 1)
                            pe.wait_ge(win_added, w + 1)
                            for k in range(KD):
                                for c in range(CG):
                                    last = nc.tensor.matmul(B_SUM[:, k * WG:(k + 1) * WG], rows[q][:, c, k * P:(k + 1) * P],
                                                            spread[0][:, c, 0:WG], start=c == 0, stop=c == CG - 1)
                            last.then_inc(win_summed, 1)

            either(pe, {"sums": sums, "linear": linear, "norm": norm, "route": route,
                        "first_items": first_items, "items": items, "last_items": last_items}, general)

        @block.scalar
        def _(act):
            act.sem_inc(sums_n_ready, 1)
            act.sem_inc(h_ready, 2 * KH)
            act.wait_ge(set1, 1)

            def sources(g, q):
                act.wait_ge(summed, g + 1)
                nc.scalar.activation(index[q][:], m["src_t"][:, bass.ds(g * CG, CG)], ACT.Copy).then_inc(index_ready, 1)

            def sums(v, part, q):
                g = v * 2 + q
                if isinstance(g, int) and g == 0:
                    sources(0, 0)
                    sources(1, 1)
                act.wait_ge(summed, g + 3)
                act.wait_ge(sums_turned, g + 1)
                nc.scalar.activation(sums_n[:], B_SUM[0:W, 0:D], ACT.Copy).then_inc(sums_n_ready, 1)
                sources(g + 2, q)

            def load_x(u, odd):
                for q in range(2):
                    t = u * 2 + q
                    if isinstance(t, int) and t == NT - 1:
                        act.dma_start(x_t[odd][q][0:LAST, :], x[t * P:N, :]).then_inc(x_in[odd][q], 16)
                    else:
                        act.dma_start(x_t[odd][q][:], x[bass.ds(t * P, P), :]).then_inc(x_in[odd][q], 16)

            def linear(u, part, odd):
                act.wait_ge(part_ready, part + 1)
                if part:
                    wait_sent(act, part - 1)
                if isinstance(u, int) and u == 0:
                    load_x(0, 0)
                if not isinstance(u, int) or u < NT // 2 - 1:
                    act.wait_ge(lin_added, u * 2 + 2)
                    load_x(u + 1, 1 - odd)
                for q in range(2):
                    t = u * 2 + q
                    act.wait_ge(lin_summed, t + 1)
                    nc.scalar.activation(sums_t[q][:], tile(t), ACT.Copy).then_inc(sums_out, 1)

            def coefficients(stage, part):
                t0, t1 = PARTS[part]
                if stage == 0:
                    act.wait_ge(lin_done, part + 1)
                    nc.scalar.activation(std[:, t0:t1], mv[:, t0:t1, 1], ACT.Sqrt, bias=m["eps"][:]).then_inc(std_ready, 1)

            def normalised(to, t):
                col = bass.ds(t, 1)
                return nc.scalar.activation(to, tile(t), ACT.Identity, bias=shift[:, col], scale=rstd[:, col])

            def norm(u, part):
                act.wait_ge(coef_ready, part + 1)
                act.wait_ge(xn_turned, u + 1)
                for q in range(2):
                    last = normalised(by_block(xn[:, q, :]), u * 2 + q)
                last.then_inc(xn_ready, 1)

            def route(stage, part):
                t0, t1 = PARTS[part]
                if stage == 1:
                    act.wait_ge(exp_ready, part + 1)
                    nc.scalar.activation(prob[:, 0:t1 - t0, :], prob[:, 0:t1 - t0, :], ACT.Exp).then_inc(exp_done, 1)
                if stage == 3:
                    act.wait_ge(routed, part + 1)

            def send_tiles(u, part, odd):
                for q in range(2):
                    t = u * 2 + q
                    if not isinstance(u, int) or u > 1:
                        act.wait_ge(sent[odd][q], u * 16 - 16 * odd)
                    normalised(by_block(send[odd][q]), t).then_inc(send_ready, 1)
                    nc.scalar.activation(send_i[odd][q][:], slot_i[:, bass.ds(t, 1), :].rearrange("p o k -> p (o k)"),
                                         ACT.Copy).then_inc(send_idx, 1)

            def load_xi(i, q, part):
                rows_of = slots_x[part][bass.ds((i - FIRST[part]) * IT, IT), :].rearrange("(b p) f -> p b f", p=P)
                act.dma_start(xi[q][:], rows_of).then_inc(xi_in[q], 16)

            def gelu(i, q):
                act.wait_ge(y_summed, i + 1)
                act.wait_ge(w1_in[q], i * 16 - 16 * q + 32)
                for j in range(KH):
                    if j % 2 == 0:
                        act.wait_ge(h_summed, i * KH + 2 * KH + j + 2)
                    nc.scalar.activation(hT[q][:, j, :], B_H[j // 2][:, j % 2 * IT:(j % 2 + 1) * IT],
                                         ACT.Gelu, bias=b1_i[q][:, j:j + 1]).then_inc(h_ready, 1)

            def first_items(_, part):
                wait_sent(act, part)
                for q in range(2):
                    load_xi(FIRST[part] + q, q, part)
                gelu(FIRST[part], 0)

            def items(v, part, q):
                i = v * 2 + q
                act.wait_ge(xi_turned, i + 1)
                load_xi(i + 2, q, part)
                gelu(i + 1, 1 - q)

            def last_items(_, part):
                gelu(FIRST[part + 1] - 1, 1)

            def slots_got(u, part):
                for q in range(2):
                    t = u * 2 + q
                    if not isinstance(u, int) or u > 0:
                        act.wait_ge(got_in[q], u * 32)
                    nc.scalar.activation(got_i[q][:], slot_i[:, bass.ds(t, 1), :].rearrange("p o k -> p (o k)"),
                                         ACT.Copy).then_inc(got_idx, 1)

            def general():
                with act.Fori(0, NG // 2) as v:
                    for q in range(2):
                        act.wait_ge(win_group, v * 2 + q + 1)
                        nc.scalar.activation(index[q][:], m["src_t"][:, bass.ds((v * 2 + q) * CG, CG)],
                                             ACT.Copy).then_inc(index_ready, 1)

            either(act, {"sums": sums, "linear": linear, "coefficients": coefficients, "norm": norm, "route": route,
                         "send": send_tiles, "first_items": first_items, "items": items, "last_items": last_items,
                         "fetch": slots_got}, general)

        @block.vector
        def _(dve):
            dve.sem_inc(in_win_ready, 1)
            dve.sem_inc(added, 1)
            dve.sem_inc(win_added, 1)
            dve.sem_inc(win_ready, 1)
            dve.sem_inc(win_group, 2)
            dve.sem_inc(lin_added, 2)
            dve.sem_inc(node_read, 1)
            dve.sem_inc(gate_read, 1)
            dve.sem_inc(xiT_ready, 2)
            dve.sem_inc(y_ready, 2)
            dve.sem_inc(res_ready, 2)
            dve.wait_ge(set1, 1)
            nc.vector.tensor_scalar(valid[:], part_iota[:], float(LAST), None, op0=ALU.is_lt)

            def spread_group(g, q):
                dve.wait_ge(summed, g + 1)
                nc.vector.tensor_copy(in_win[q][:], m["dst_rel"][:, bass.ds(g * CG, CG)]).then_inc(in_win_ready, 1)
                dve.wait_ge(in_win_ready, g + 2)
                for c in range(CG):
                    last = nc.vector.tensor_scalar(spread[q][:, c, :], m["iota_w"][:], in_win[q][:, c:c + 1],
                                                   m["wgt"][:, bass.ds(g * CG + c, 1)], op0=ALU.is_equal, op1=ALU.mult)
                last.then_inc(spread_ready, 1)

            def add_group(g):
                base = dve.value_load(m["base_i"][:, bass.ds(g, 1)], min_val=0, max_val=N - 1)
                here = acc[:, :, bass.ds(base, W)]
                dve.wait_ge(sums_turned, g + 2)
                dve.wait_ge(added, g + 1)
                nc.vector.tensor_tensor(here, here, B_TURN[:, 0:KD * W].rearrange("p (k w) -> p k w", k=KD),
                                        op=ALU.add).then_inc(added, 1)

            def sums(v, part, q):
                g = v * 2 + q
                if isinstance(g, int) and g == 0:
                    spread_group(0, 0)
                spread_group(g + 1, 1 - q)
                add_group(g)

            def linear(u, part, odd):
                for q in range(2):
                    t = u * 2 + q
                    dve.wait_ge(x_in[odd][q], u * 8 + 16 - 8 * odd)
                    nc.vector.tensor_tensor(x_t[odd][q][:], x_t[odd][q][:], m["gnn_bB"][:], op=ALU.add).then_inc(x_biased, 1)
                for q in range(2):
                    t = u * 2 + q
                    dve.wait_ge(x_biased, t + 1)
                    dve.wait_ge(lin_summed, t + 3)
                    nc.vector.tensor_tensor(tile(t), by_block((B_NODE, B_GATE)[q][:, 0:D]), by_block(x_t[odd][q][:]),
                                            op=ALU.add).then_inc(lin_added, 1)
                dve.wait_ge(lin_added, u * 2 + 4)
                for q in range(2):
                    t = u * 2 + q
                    dve.sem_inc(lin_seen, 1)
                    nc.vector.bn_stats(bn6[q][:], tile(t)).then_inc(lin_stats, 1)
                for q in range(2):
                    t = u * 2 + q
                    dve.wait_ge(lin_stats, t + 1)
                    dve.sem_inc(lin_seen, 1)
                    last = nc.vector.bn_aggr(mv2[:, q, :], bn6[q][:])
                last.then_inc(lin_aggr, 1)
                dve.wait_ge(lin_aggr, u + 1)
                nc.vector.tensor_copy(mv[:, bass.ds(u * 2, 2), :], mv2[:]).then_inc(lin_kept, 1)

            def coefficients(stage, part):
                t0, t1 = PARTS[part]
                if stage == 0:
                    dve.wait_ge(lin_kept, t1 // 2)
                    dve.sem_inc(lin_done, 1)
                else:
                    dve.wait_ge(std_ready, part + 1)
                    then(nc.vector.reciprocal(rstd[:, t0:t1], std[:, t0:t1]))
                    nc.vector.scalar_tensor_tensor(shift[:, t0:t1], mv[:, t0:t1, 0], -1.0, rstd[:, t0:t1],
                                                   op0=ALU.mult, op1=ALU.mult).then_inc(coef_ready, 1)

            def norm(u, part):
                dve.wait_ge(xn_turned, u + 2)
                dve.wait_ge(logits_done, u + 1)
                nc.vector.tensor_copy(xnT[:].rearrange("p q k j -> p (q k j)"), B_NODE[:]).then_inc(xnT_ready, 1)
                dve.wait_ge(xnT_ready, u + 1)
                dve.sem_inc(node_read, 1)
                dve.wait_ge(logits_done, u + 2)
                nc.vector.tensor_tensor(prob[:, bass.ds(u * 2 - PARTS[part][0], 2), :],
                                        B_GATE[:, 0:2 * NX].rearrange("p (q e) -> p q e", q=2),
                                        m["gate_bB"][:].unsqueeze(1).to_broadcast([P, 2, NX]),
                                        op=ALU.add).then_inc(gate_read, 1)

            steps = [0]

            def then(instruction):
                instruction.then_inc(route_step, 1)
                steps[0] += 1
                dve.wait_ge(route_step, steps[0])

            def route(stage, part):
                t0, t1 = PARTS[part]
                n = t1 - t0
                pr, m1, m2, cd, bo, ps = (a[:, 0:n, :] for a in (prob, mask1, mask2, cand, both, pos))
                per_tile = lambda a: a[:, 0:n].unsqueeze(2).to_broadcast([P, n, NX])
                per_expert = lambda a: a[:].unsqueeze(1).to_broadcast([P, n, NX])
                counts = count_et[:, :, 0:n]
                upto = upto_et[:, :, 0:n]
                if stage == 0:
                    dve.wait_ge(gate_read, t1 // 2 + part + 1)
                    then(nc.vector.tensor_reduce(top[:, 0:n], pr, axis=AX.X, op=ALU.max))
                    nc.vector.tensor_tensor(pr, pr, per_tile(top), op=ALU.subtract).then_inc(exp_ready, 1)
                if stage == 1:
                    dve.wait_ge(exp_done, part + 1)
                    then(nc.vector.tensor_reduce(top[:, 0:n], pr, axis=AX.X, op=ALU.add))
                    then(nc.vector.reciprocal(top_r[:, 0:n], top[:, 0:n]))
                    then(nc.vector.tensor_tensor(pr, pr, per_tile(top_r), op=ALU.mult))
                    for k, mk in enumerate((m1, m2)):
                        then(nc.vector.tensor_reduce(weight[:, t0:t1, k], pr, axis=AX.X, op=ALU.max))
                        then(nc.vector.tensor_tensor(cd, pr, weight[:, t0:t1, k:k + 1].to_broadcast([P, n, NX]), op=ALU.is_equal))
                        then(nc.vector.tensor_tensor(cd, cd, per_expert(rev), op=ALU.mult))
                        then(nc.vector.tensor_reduce(top[:, 0:n], cd, axis=AX.X, op=ALU.max))
                        then(nc.vector.tensor_tensor(mk, cd, per_tile(top), op=ALU.is_equal))
                        if k == 0:
                            then(nc.vector.scalar_tensor_tensor(pr, m1, -2.0, pr, op0=ALU.mult, op1=ALU.add))
                    if t1 == NT:
                        for mk in (m1, m2):
                            then(nc.vector.tensor_scalar(mk[:, n - 1, :], mk[:, n - 1, :], valid[:], None, op0=ALU.mult))
                    nc.vector.tensor_tensor(bo, m1, m2, op=ALU.add).then_inc(mask_ready, 1)
                if stage == 2:
                    dve.wait_ge(ranked, part + 1)
                    flat = lambda a: a[:].rearrange("p e t -> p (e t)")
                    then(nc.vector.tensor_copy(counts, B_GATE[:, n * NX:2 * n * NX].rearrange("p (t e) -> p e t", e=NX)))
                    if n < NTM:
                        then(nc.vector.memset(count_et[:, :, n:], 0.0))
                    then(nc.vector.tensor_tensor_scan(flat(upto_et), flat(keep_et), flat(count_et), 0.0, op0=ALU.mult, op1=ALU.add))
                    total = upto_et[:, :, n - 1]
                    then(nc.vector.tensor_scalar(cnt_i[:], total, float(IT - 1), None, op0=ALU.add))
                    then(nc.vector.tensor_scalar(items_i[:], cnt_i[:], IT.bit_length() - 1, None, op0=ALU.arith_shift_right))
                    then(nc.vector.tensor_copy(items_f[:], items_i[:]))
                    then(nc.vector.tensor_tensor_scan(upto_f[:], ones[:, 0:NX], items_f[:], 0.0, op0=ALU.mult, op1=ALU.add))
                    then(nc.vector.tensor_tensor(first_f[:], upto_f[:], items_f[:], op=ALU.subtract))
                    then(nc.vector.tensor_scalar(first_f[:], first_f[:], float(IT), None, op0=ALU.mult))
                    then(nc.vector.tensor_tensor(upto, upto, counts, op=ALU.subtract))
                if stage == 3:
                    then(nc.vector.tensor_tensor(ps, upto.rearrange("p e t -> p t e"), per_expert(first_f), op=ALU.add))
                    then(nc.vector.tensor_tensor(ps, ps, B_GATE[:, 0:n * NX].rearrange("p (t e) -> p t e", e=NX), op=ALU.add))
                    dve.sem_inc(gate_read, 1)
                    for k, mk in enumerate((m1, m2)):
                        then(nc.vector.tensor_tensor(cd, mk, ps, op=ALU.mult))
                        then(nc.vector.tensor_reduce(slot_f[:, 0:n, k], cd, axis=AX.X, op=ALU.add))
                    then(nc.vector.tensor_copy(slot_i[:, t0:t1, :], slot_f[:, 0:n, :]))
                    ni, i0 = ITEMS[part], FIRST[part]
                    then(nc.vector.tensor_scalar(item_f[1][:, 0:ni], item_iota[:, 0:ni], upto_f[0:1, 0:1], None, op0=ALU.is_ge))
                    for e in range(1, NX - 1):
                        then(nc.vector.scalar_tensor_tensor(item_f[1 - e % 2][:, 0:ni], item_iota[:, 0:ni], upto_f[0:1, e:e + 1],
                                                            item_f[e % 2][:, 0:ni], op0=ALU.is_ge, op1=ALU.add))
                    then(nc.vector.tensor_copy(item_e[:, i0:i0 + ni], item_f[1 - (NX - 2) % 2][:, 0:ni]))
                    dve.sem_inc(routed, 1)

            def turned_items(i, q):
                dve.wait_ge(xi_turned, i + 1)
                dve.wait_ge(h_summed, i * KH + KH)
                nc.vector.tensor_copy(xiT[q][:].rearrange("p k j -> p (k j)"), B_XI[:]).then_inc(xiT_ready, 1)

            def results(i, q):
                dve.wait_ge(w2_in[q], i * 16 - 16 * q + 32)
                if not isinstance(i, int) or i > 1:
                    dve.wait_ge(y_out[q], i * 8 - 8 * q)
                dve.wait_ge(y_summed, i + 3)
                nc.vector.tensor_tensor(y_i[q][:], B_Y[:].rearrange("p (b f) -> p b f", b=TB),
                                        b2_i[q][:].unsqueeze(1).to_broadcast([P, TB, D]), op=ALU.add).then_inc(y_ready, 1)

            def first_items(_, part):
                for q in range(2):
                    turned_items(FIRST[part] + q, q)

            def items(v, part, q):
                turned_items(v * 2 + q + 2, q)
                results(v * 2 + q, q)

            def last_items(_, part):
                for q in range(2):
                    results(FIRST[part + 1] - 2 + q, q)

            def combine(u, part):
                for q in range(2):
                    t = u * 2 + q
                    dve.wait_ge(got_in[q], u * 32 + 32)
                    nc.vector.scalar_tensor_tensor(by_block(got[q][:, 0, :]), by_block(got[q][:, 0, :]),
                                                   weight[:, bass.ds(t, 1), 0:1].rearrange("p o k -> p (o k)"),
                                                   tile(t), op0=ALU.mult, op1=ALU.add).then_inc(got_half, 1)
                for q in range(2):
                    t = u * 2 + q
                    dve.wait_ge(got_half, t + 1)
                    if not isinstance(u, int) or u > 0:
                        dve.wait_ge(res_out[q], u * 16)
                    nc.vector.scalar_tensor_tensor(res[q][:], got[q][:, 1, :],
                                                   weight[:, bass.ds(t, 1), 1:2].rearrange("p o k -> p (o k)"),
                                                   got[q][:, 0, :], op0=ALU.mult, op1=ALU.add).then_inc(res_ready, 1)

            def ready(pairs, part):
                if pairs:
                    dve.wait_ge(added, pairs * 2 + 1)
                dve.sem_inc(part_ready, 1)

            def general():
                steps[0] = 0
                with dve.Fori(0, NG // 2) as v:
                    for q in range(2):
                        g = v * 2 + q
                        w0 = dve.value_load(win_start[:, bass.ds(g, 1)], min_val=0, max_val=MAX_WINDOWS)
                        w1 = dve.value_load(win_start[:, bass.ds(g + 1, 1)], min_val=1, max_val=MAX_WINDOWS)
                        base = dve.value_load(m["base_i"][:, bass.ds(g, 1)], min_val=0, max_val=N - 1)
                        dve.wait_ge(win_ready, w0 + g + 1)
                        nc.vector.tensor_copy(in_win[0][:], m["dst_rel"][:, bass.ds(g * CG, CG)]).then_inc(win_ready, 1)
                        with dve.Fori(w0, w1) as w:
                            dve.wait_ge(win_ready, w + g + 2)
                            for c in range(CG):
                                last = nc.vector.tensor_scalar(spread[0][:, c, 0:WG], m["iota_w"][:, 0:WG], in_win[0][:, c:c + 1],
                                                               m["wgt"][:, bass.ds(g * CG + c, 1)],
                                                               op0=ALU.is_equal, op1=ALU.mult)
                            last.then_inc(win_spread, 1)
                            dve.wait_ge(win_spread, w + 1)
                            nc.vector.tensor_scalar(in_win[0][:], in_win[0][:], float(WG), None, op0=ALU.subtract).then_inc(win_ready, 1)
                            dve.wait_ge(win_summed, w + 1)
                            dve.wait_ge(win_added, w + 1)
                            at = nc.s_assert_within(base + (w - w0) * WG, 0, NPAD,
                                                    skip_runtime_bounds_check_because="the window holds a node below N")
                            here = acc[:, :, bass.ds(at, WG)]
                            nc.vector.tensor_tensor(here, here, B_SUM[:, 0:KD * WG].rearrange("p (k w) -> p k w", k=KD),
                                                    op=ALU.add).then_inc(win_added, 1)
                        dve.sem_inc(win_group, 1)
                windows = dve.value_load(win_start[:, NG:NG + 1], min_val=1, max_val=MAX_WINDOWS)
                dve.wait_ge(win_added, windows + 1)
                dve.sem_inc(win_group, 1)

            either(dve, {"sums": sums, "ready": ready, "linear": linear, "coefficients": coefficients, "norm": norm,
                         "route": route, "first_items": first_items, "items": items, "last_items": last_items,
                         "combine": combine}, general)


_INS = ["x", "src", "dst", "edge_weight", "L0_gnn_W", "L0_gnn_b", "L0_ffn_gate_w", "L0_ffn_gate_b",
        "L0_ffn_W1", "L0_ffn_b1", "L0_ffn_W2", "L0_ffn_b2"]


def kernel(**inputs):
    import numpy as np
    import concourse.bacc as bacc
    from concourse.bass_utils import run_bass_kernel_spmd

    nc = bacc.Bacc("TRN2", target_bir_lowering=False, num_devices=1)
    arrays, args = {}, []
    for name in _INS:
        a = np.ascontiguousarray(inputs[name])
        arrays["in_" + name] = a
        args.append(nc.dram_tensor("in_" + name, a.shape, mybir.dt.from_np(a.dtype), kind="ExternalInput").ap())
    out = nc.dram_tensor("out_nodes", (N, D), F32, kind="ExternalOutput").ap()
    build(nc, *args, out)
    return run_bass_kernel_spmd(nc, [arrays], core_ids=[0]).results[0]["out_nodes"]
```
